# Optimizing a Trainium2 kernel written in Bass

```python
import numpy as np
import jax
import jax.numpy as jnp

def _softmax(x, axis=-1):
    return jax.nn.softmax(x, axis=axis)

def _gelu(x):
    return jax.nn.gelu(x, approximate=True)

def _silu(x):
    return jax.nn.silu(x)

def _sigmoid(x):
    return jax.nn.sigmoid(x)

def _layernorm(x, axis=-1, eps=1e-05):
    m = jnp.mean(x, axis=axis, keepdims=True)
    v = jnp.var(x, axis=axis, keepdims=True)
    return (x - m) / jnp.sqrt(v + eps)

def _scatter_add(tgt, idx, src, axis=0):
    return tgt.at[idx].add(src)

def _segment_sum(src, seg, n):
    return jax.ops.segment_sum(src, seg, n)
kernel_name = 'mk_cond_seq_d1_seqx_r4_266024'

def setup_inputs(seed: int=0):
    np.random.seed(seed)
    _w = jnp.asarray

    def _rec_inputs():
        import jax
        import jax.numpy as jnp
        _rk = jax.random.key(seed)
        x = 7.22e-05 + 1 * jax.random.normal(jax.random.fold_in(_rk, 1), (8, 256, 256), jnp.float32)
        _lenS = 256 - jax.random.randint(jax.random.fold_in(_rk, 7), (8,), 0, max(1, 256 // 4) + 1, jnp.int32)
        _lenS2 = 256 - jax.random.randint(jax.random.fold_in(_rk, 8), (8,), 0, max(1, 256 // 4) + 1, jnp.int32)
        cond_1024 = 0.0061147 + 1.02565 * jax.random.normal(jax.random.fold_in(_rk, 11), (8, 256), jnp.float32)
        return (x, cond_1024)
    x, cond_1024 = _rec_inputs()

    def _L0_cond_setup():
        import jax, jax.numpy as jnp
        import numpy as np
        DIM = 256
        FF_MULT = 2
        EPS = 1e-06

        def _ln(x):
            mu = jnp.mean(x, axis=-1, keepdims=True)
            var = jnp.mean(jnp.square(x - mu), axis=-1, keepdims=True)
            return (x - mu) * jax.lax.rsqrt(var + EPS)
        key = jax.random.key(seed)
        ks = jax.random.split(key, 12)
        b, n, d = (4, 512, DIM)
        h = FF_MULT * d
        s = lambda fan_in: 1.0 / np.sqrt(fan_in)
        return {'x': jax.random.normal(ks[0], (b, n, d), jnp.float32), 't': jax.random.normal(ks[1], (b, d), jnp.float32), 'ada_w': jax.random.normal(ks[2], (d, 6 * d), jnp.float32) * s(d), 'ada_b': jnp.zeros((6 * d,), jnp.float32), 'ssm_w1': jax.random.normal(ks[3], (d, d), jnp.float32) * s(d), 'ssm_b1': jnp.zeros((d,), jnp.float32), 'ssm_w2': jax.random.normal(ks[4], (d, d), jnp.float32) * s(d), 'ssm_b2': jnp.zeros((d,), jnp.float32), 'ff_w1': jax.random.normal(ks[5], (d, h), jnp.float32) * s(d), 'ff_b1': jnp.zeros((h,), jnp.float32), 'ff_w2': jax.random.normal(ks[6], (h, d), jnp.float32) * s(h), 'ff_b2': jnp.zeros((d,), jnp.float32)}
    _L0_cond_all = _L0_cond_setup()
    _L0_cond_in = {k: v for k, v in _L0_cond_all.items() if k in ('ada_w', 'ada_b', 'ssm_w1', 'ssm_b1', 'ssm_w2', 'ssm_b2', 'ff_w1', 'ff_b1', 'ff_w2', 'ff_b2')}
    del _L0_cond_all
    return {'x': x, 'cond_1024': cond_1024, 'L0_cond_ada_w': _L0_cond_in['ada_w'], 'L0_cond_ada_b': _L0_cond_in['ada_b'], 'L0_cond_ssm_w1': _L0_cond_in['ssm_w1'], 'L0_cond_ssm_b1': _L0_cond_in['ssm_b1'], 'L0_cond_ssm_w2': _L0_cond_in['ssm_w2'], 'L0_cond_ssm_b2': _L0_cond_in['ssm_b2'], 'L0_cond_ff_w1': _L0_cond_in['ff_w1'], 'L0_cond_ff_b1': _L0_cond_in['ff_b1'], 'L0_cond_ff_w2': _L0_cond_in['ff_w2'], 'L0_cond_ff_b2': _L0_cond_in['ff_b2']}

def reference(x, cond_1024, L0_cond_ada_w, L0_cond_ada_b, L0_cond_ssm_w1, L0_cond_ssm_b1, L0_cond_ssm_w2, L0_cond_ssm_b2, L0_cond_ff_w1, L0_cond_ff_b1, L0_cond_ff_w2, L0_cond_ff_b2):
    import jax
    import jax.numpy as jnp

    def _L0_cond_ref(x, t, ada_w, ada_b, ssm_w1, ssm_b1, ssm_w2, ssm_b2, ff_w1, ff_b1, ff_w2, ff_b2):
        import jax, jax.numpy as jnp
        import numpy as np
        DIM = 256
        FF_MULT = 2
        EPS = 1e-06

        def _ln(x):
            mu = jnp.mean(x, axis=-1, keepdims=True)
            var = jnp.mean(jnp.square(x - mu), axis=-1, keepdims=True)
            return (x - mu) * jax.lax.rsqrt(var + EPS)
        emb = jnp.dot(jax.nn.silu(t), ada_w) + ada_b
        shift_msa, scale_msa, gate_msa, shift_mlp, scale_mlp, gate_mlp = jnp.split(emb, 6, axis=-1)
        norm = _ln(x) * (1.0 + scale_msa[:, None]) + shift_msa[:, None]
        h = jax.nn.gelu(jnp.dot(norm, ssm_w1) + ssm_b1, approximate=False)
        ssm_out = jnp.dot(h, ssm_w2) + ssm_b2
        x = x + gate_msa[:, None] * ssm_out
        norm2 = _ln(x) * (1.0 + scale_mlp[:, None]) + shift_mlp[:, None]
        hf = jax.nn.gelu(jnp.dot(norm2, ff_w1) + ff_b1, approximate=True)
        ff_out = jnp.dot(hf, ff_w2) + ff_b2
        x = x + gate_mlp[:, None] * ff_out
        return x
    x = _L0_cond_ref(x, cond_1024, L0_cond_ada_w, L0_cond_ada_b, L0_cond_ssm_w1, L0_cond_ssm_b1, L0_cond_ssm_w2, L0_cond_ssm_b2, L0_cond_ff_w1, L0_cond_ff_b1, L0_cond_ff_w2, L0_cond_ff_b2)
    return x

_drawn_inputs = setup_inputs


def setup_inputs(seed=0):
    import zlib

    import numpy as np

    out = dict(_drawn_inputs(seed))
    spreads = {'L0_cond_ada_b': (0.0, 0.1),
     'L0_cond_ssm_b1': (0.0, 0.1),
     'L0_cond_ssm_b2': (0.0, 0.1),
     'L0_cond_ff_b1': (0.0, 0.1),
     'L0_cond_ff_b2': (0.0, 0.1)}
    factors = {}
    for name, (base, spread) in spreads.items():
        noise = np.random.default_rng([zlib.crc32(name.encode()), seed]).standard_normal(out[name].shape)
        drawn = base * np.exp(spread * noise) if base else spread * noise
        out[name] = jnp.asarray(drawn.astype(out[name].dtype))
    for name, factor in factors.items():
        out[name] = (out[name] * factor).astype(out[name].dtype)
    return out
```

```python
from contextlib import ExitStack

import concourse.bass as bass
from concourse import mybir

ALU = mybir.AluOpType
ACT = mybir.ActivationFunctionType
F32 = mybir.dt.float32
F32R = mybir.dt.float32r

P = 128
EPS = 1e-6
HALVES = 2


def conditioned_block_kernel(
    nc: bass.Bass,
    x: bass.AP,
    cond: bass.AP,
    ada_w: bass.AP,
    ada_b: bass.AP,
    w1: bass.AP,
    b1: bass.AP,
    w2: bass.AP,
    b2: bass.AP,
    ff_w1: bass.AP,
    ff_b1: bass.AP,
    ff_w2: bass.AP,
    ff_b2: bass.AP,
    gate_scratch: bass.AP,
    out: bass.AP,
):
    B, S, D = x.shape
    KD = D // P
    CT = S // P
    NG = B // HALVES
    TILES = HALVES * CT
    GT = TILES * P
    HT = CT * P
    HIDDEN = (w1.shape[1], ff_w1.shape[1])
    M = tuple(h // P for h in HIDDEN)
    MMAX = max(M)
    PAIRS = MMAX // 2
    LAST = 2 * NG - 1
    assert (S, D, GT, HIDDEN) == (256, 256, 512, (256, 512))

    NB_ADA = ada_b.shape[0] // P
    ROW_B1 = (NB_ADA, NB_ADA + M[0])
    ROWS = NB_ADA + M[0] + M[1]
    ADA_LAYER = 3 * KD

    with ExitStack() as ctx:
        def sb(name, shape, dt=F32):
            return ctx.enter_context(nc.sbuf_tensor(name, shape, dt))

        def psum(name, shape):
            return ctx.enter_context(nc.psum_tensor(name, shape, F32))

        def sem(name):
            return ctx.enter_context(nc.semaphore(name))

        xres = sb("xres", [P, NG, TILES, D])
        xhat = sb("xhat", [P, TILES, D])
        stats = sb("stats", [P, TILES, 6])
        meanvar = sb("meanvar", [P, TILES, 2])
        vareps = sb("vareps", [P, TILES])
        rstd = sb("rstd", [P, TILES])
        minus_half = sb("minus_half", [P, TILES])
        ident = sb("ident", [P, P])

        norm = sb("norm", [P, KD, GT])
        norm_hi = sb("norm_hi", [P, KD, GT], F32R)
        norm_lo = sb("norm_lo", [P, KD, GT], F32R)
        h = sb("h", [P, MMAX, GT])
        h_hi = sb("h_hi", [P, MMAX, GT], F32R)
        h_lo = sb("h_lo", [P, MMAX, GT], F32R)
        branch = sb("branch", [P, HALVES, CT, D])

        w_up = [sb(f"w_up{n}", [P, KD, HIDDEN[n]]) for n in range(2)]
        w_up_hi = [sb(f"w_up_hi{n}", [P, KD, HIDDEN[n]], F32R) for n in range(2)]
        w_up_lo = [sb(f"w_up_lo{n}", [P, KD, HIDDEN[n]], F32R) for n in range(2)]
        w_down = [sb(f"w_down{n}", [P, M[n], D]) for n in range(2)]
        w_down_hi = [sb(f"w_down_hi{n}", [P, M[n], D], F32R) for n in range(2)]
        w_down_lo = [sb(f"w_down_lo{n}", [P, M[n], D], F32R) for n in range(2)]

        cond_rows = sb("cond_rows", [B, D])
        cond_silu = sb("cond_silu", [P, KD, B])
        ada_sb = sb("ada_sb", [P, KD, 2, 3 * D])
        bias_rows = sb("bias_rows", [ROWS, P])
        bias_cols = sb("bias_cols", [P, ROWS])
        shift_scale = [sb(f"shift_scale{n}", [P, 2, KD, B]) for n in range(2)]
        gate_bias = sb("gate_bias", [B, 2, D])
        gate_rows = sb("gate_rows", [B, 2, D])
        gate = [sb(f"gate{n}", [P, B, D]) for n in range(2)]
        down_bias = [sb(f"down_bias{n}", [P, D]) for n in range(2)]
        warm = sb("warm", [P, 1])

        ps_tr = [psum(f"ps_tr{k}", [P, GT]) for k in range(KD)]
        ps_up = [psum(f"ps_up{m}", [P, GT]) for m in range(MMAX)]
        ps_down = [psum(f"ps_down{hb}", [P, CT, D]) for hb in range(HALVES)]
        ps_cond, ps_bias = ps_down
        ps_mod = [ps_up[3], ps_up[2]]
        ps_gate = ps_down[0]

        cond_loaded = sem("cond_loaded")
        biases_loaded = sem("biases_loaded")
        gate_bias_loaded = sem("gate_bias_loaded")
        ada_loaded = [sem(f"ada_loaded{n}") for n in range(2)]
        x_first_loaded = sem("x_first_loaded")
        x_rest_loaded = sem("x_rest_loaded")
        w_up_loaded = [sem(f"w_up_loaded{n}") for n in range(2)]
        w_down_loaded = [sem(f"w_down_loaded{n}") for n in range(2)]
        down_bias_loaded = sem("down_bias_loaded")
        gates_stored = sem("gates_stored")
        gates_loaded = [sem(f"gates_loaded{n}") for n in range(2)]
        out_stored = sem("out_stored")

        ident_zeroed = sem("ident_zeroed")
        ident_ready = sem("ident_ready")
        constants_ready = sem("constants_ready")
        cond_transposed = sem("cond_transposed")
        bias_transposed = sem("bias_transposed")
        silu_ready = sem("silu_ready")
        bias_ready = sem("bias_ready")
        mod_summed = sem("mod_summed")
        mod_ready = sem("mod_ready")
        gates_ready = sem("gates_ready")

        stats_done = sem("stats_done")
        meanvar_done = sem("meanvar_done")
        vareps_done = sem("vareps_done")
        rstd_done = sem("rstd_done")
        xhat_ready = sem("xhat_ready")
        transposed = sem("transposed")
        norm_ready = sem("norm_ready")
        norm_hi_ready = sem("norm_hi_ready")
        norm_lo_ready = sem("norm_lo_ready")
        up_done = [sem(f"up_done{m}") for m in range(MMAX)]
        gelu_done = [sem(f"gelu_done{m}") for m in range(MMAX)]
        h_hi_ready = [sem(f"h_hi_ready{q}") for q in range(PAIRS)]
        h_lo_ready = [sem(f"h_lo_ready{q}") for q in range(PAIRS)]
        down_done = sem("down_done")
        biased = sem("biased")
        gated = sem("gated")
        residual_done = sem("residual_done")
        w_up_hi_ready = [sem(f"w_up_hi_ready{n}") for n in range(2)]
        w_up_lo_ready = [sem(f"w_up_lo_ready{n}") for n in range(2)]
        w_down_hi_ready = [sem(f"w_down_hi_ready{n}") for n in range(2)]
        w_down_lo_ready = [sem(f"w_down_lo_ready{n}") for n in range(2)]

        def group(layer, i):
            return i - layer * NG

        def runs(chunk, i):
            return i if chunk < M[0] else i - NG

        block = ctx.enter_context(nc.Block())

        @block.sync
        def _(sp):
            def load_x(g, signal):
                sp.dma_start(xres[:, g].rearrange("p (b c) f -> p b (c f)", b=HALVES),
                             x[HALVES * g:HALVES * (g + 1)].rearrange("b (p c) f -> p b (c f)", c=CT)
                             ).then_inc(signal, 16)

            def load_w(dst, w, signal):
                sp.dma_start(dst[:, :, :], w.rearrange("(k p) n -> p k n", p=P)).then_inc(signal, 16)

            sp.dma_start(cond_rows[:, :], cond).then_inc(cond_loaded, 16)
            load_x(0, x_first_loaded)
            load_w(w_up[0], w1, w_up_loaded[0])
            load_x(1, x_rest_loaded)
            load_w(w_down[0], w2, w_down_loaded[0])
            for g in range(2, NG):
                load_x(g, x_rest_loaded)
            load_w(w_up[1], ff_w1, w_up_loaded[1])
            load_w(w_down[1], ff_w2, w_down_loaded[1])

            sp.wait_ge(gates_ready, 1)
            sp.dma_start(gate_scratch, gate_rows[:, :, :]).then_inc(gates_stored, 16)
            sp.wait_ge(gates_stored, 16)
            for n in range(2):
                sp.dma_start(gate[n][:, :, :],
                             gate_scratch[:, n, :].rearrange("(a b) f -> a b f", a=1).to_broadcast([P, B, D])
                             ).then_inc(gates_loaded[n], 16)
            for i in range(NG, LAST + 1):
                for hb in range(HALVES):
                    b = HALVES * group(1, i) + hb
                    sp.wait_ge(residual_done, HALVES * i + hb + 1)
                    sp.dma_start(out[b].rearrange("(p c) f -> p (c f)", c=CT),
                                 xres[:, group(1, i), CT * hb:CT * (hb + 1), :].rearrange("p c f -> p (c f)")
                                 ).then_inc(out_stored, 16)
            sp.wait_ge(out_stored, 16 * B)

        @block.scalar
        def _(act):
            act.dma_start(bias_rows[0:NB_ADA, :], ada_b.rearrange("(r p) -> r p", p=P)).then_inc(biases_loaded, 16)
            act.dma_start(bias_rows[ROW_B1[0]:ROW_B1[1], :], b1.rearrange("(r p) -> r p", p=P)).then_inc(biases_loaded, 16)
            act.dma_start(bias_rows[ROW_B1[1]:ROWS, :], ff_b1.rearrange("(r p) -> r p", p=P)).then_inc(biases_loaded, 16)
            ada_v = ada_w.rearrange("(k p) (l n) -> p k l n", p=P, l=2)
            for n in range(2):
                act.dma_start(ada_sb[:, :, n, :], ada_v[:, :, n, :]).then_inc(ada_loaded[n], 16)
            act.dma_start(gate_bias[:, :, :],
                          ada_b.rearrange("(a l n) -> a l n", a=1, l=2)[:, :, 2 * D:3 * D].to_broadcast([B, 2, D])
                          ).then_inc(gate_bias_loaded, 16)
            for n, b in enumerate((b2, ff_b2)):
                act.dma_start(down_bias[n][:, :], b.rearrange("(a f) -> a f", a=1).to_broadcast([P, D])
                              ).then_inc(down_bias_loaded, 16)

            act.wait_ge(cond_transposed, 1)
            act.activation(cond_silu[:, :, :].rearrange("p k b -> p (k b)"),
                           ps_cond[:, 0, 0:KD * B], ACT.Silu).then_inc(silu_ready, 1)
            act.wait_ge(constants_ready, 1)
            act.activation(warm[:, :], minus_half[:, 0:1], ACT.Gelu)

            def modulate(layer, i):
                for k in range(KD):
                    act.wait_ge(transposed, KD * i + k + 1)
                    act.wait_ge(norm_lo_ready, KD * (i - 1) + k + 1) if not (isinstance(i, int) and i == 0) else None
                    for hb in range(HALVES):
                        b = HALVES * group(layer, i) + hb
                        cols = slice(HT * hb, HT * (hb + 1))
                        act.activation(norm[:, k, cols], ps_tr[k][:, cols], ACT.Identity,
                                       bias=shift_scale[layer][:, 0, k, bass.ds(b, 1)],
                                       scale=shift_scale[layer][:, 1, k, bass.ds(b, 1)]).then_inc(norm_ready, 1)

            def gelu(layer, i, first):
                func = (ACT.Gelu, ACT.Gelu_apprx_tanh)[layer]
                for m in range(M[layer]):
                    act.wait_ge(up_done[m], runs(m, i) + 1)
                    if not first[m]:
                        act.wait_ge(h_lo_ready[m // 2], HALVES * runs(m, i))
                    row = ROW_B1[layer] + m
                    act.activation(h[:, m, :], ps_up[m][:, :], func,
                                   bias=bias_cols[:, row:row + 1]).then_inc(gelu_done[m], 1)

            act.wait_ge(mod_ready, 2)
            for i in range(2):
                modulate(0, i)
                gelu(0, i, [i == 0] * MMAX)
            with act.Fori(2, NG) as i:
                modulate(0, i)
                gelu(0, i, [False] * MMAX)
            act.wait_ge(mod_ready, 4)
            act.activation(warm[:, :], minus_half[:, 0:1], ACT.Gelu_apprx_tanh)
            modulate(1, NG)
            gelu(1, NG, [False] * M[0] + [True] * (MMAX - M[0]))
            with act.Fori(NG + 1, LAST + 1) as i:
                modulate(1, i)
                gelu(1, i, [False] * MMAX)

        @block.vector
        def _(dve):
            def ln_stats(layer, i):
                g = group(layer, i)
                if layer == 1:
                    dve.wait_ge(residual_done, HALVES * (g + 1))
                for t in range(TILES):
                    dve.bn_stats(stats[:, t, :], xres[:, bass.ds(g, 1), t, :].rearrange("p a f -> p (a f)")
                                 ).then_inc(stats_done, 1)
                for t in range(TILES):
                    dve.wait_ge(stats_done, TILES * i + t + 1)
                    dve.bn_aggr(meanvar[:, t, :], stats[:, t, :]).then_inc(meanvar_done, 1)
                dve.wait_ge(meanvar_done, TILES * (i + 1))
                dve.tensor_scalar(vareps[:, :], meanvar[:, :, 1], EPS, None, ALU.add).then_inc(vareps_done, 1)

            def ln_apply(layer, i, first=False):
                g = group(layer, i)
                dve.wait_ge(rstd_done, i + 1)
                if not first:
                    dve.wait_ge(transposed, KD * i)
                for t in range(TILES):
                    dve.tensor_scalar(xhat[:, t, :], xres[:, bass.ds(g, 1), t, :].rearrange("p a f -> p (a f)"),
                                      meanvar[:, t, 0:1], rstd[:, t:t + 1],
                                      ALU.subtract, ALU.mult).then_inc(xhat_ready, 1)

            def split_norm(i, first=False):
                for k in range(KD):
                    dve.wait_ge(norm_ready, HALVES * (KD * i + k + 1))
                    if not first:
                        dve.wait_ge(up_done[M[0] - 1], i)
                    dve.tensor_copy(norm_hi[:, k, :], norm[:, k, :]).then_inc(norm_hi_ready, 1)

            def split_h(layer, i, hb, first=False):
                cols = slice(HT * hb, HT * (hb + 1))
                for q in range(M[layer] // 2):
                    dve.wait_ge(gelu_done[2 * q + 1], runs(2 * q, i) + 1)
                    if not first:
                        dve.wait_ge(down_done, HALVES * (i - 1) + hb + 1)
                    dve.tensor_copy(h_hi[:, 2 * q:2 * q + 2, cols], h[:, 2 * q:2 * q + 2, cols]
                                    ).then_inc(h_hi_ready[q], 1)

            def add_bias(layer, i, hb, first=False):
                dve.wait_ge(down_done, HALVES * i + hb + 1)
                if not first:
                    dve.wait_ge(residual_done, HALVES * (i - 1) + hb + 1)
                dve.tensor_tensor(branch[:, hb, :, :], ps_down[hb][:, :, :],
                                  down_bias[layer][:, :].rearrange("p (a f) -> p a f", a=1).to_broadcast([P, CT, D]),
                                  ALU.add).then_inc(biased, 1)

            def split_weight(dst, src, loaded, ready):
                dve.wait_ge(loaded, 16)
                dve.tensor_copy(dst[:, :, :], src[:, :, :]).then_inc(ready, 1)

            def modulation(layer):
                dve.wait_ge(mod_summed, layer + 1)
                ps = ps_mod[layer][:, 0:2 * KD * B].rearrange("p (s k b) -> p s k b", s=2, k=KD)
                r = ADA_LAYER * layer
                dve.tensor_tensor(shift_scale[layer][:, 0], ps[:, 0],
                                  bias_cols[:, r:r + KD].rearrange("p (k a) -> p k a", a=1).to_broadcast([P, KD, B]),
                                  ALU.add).then_inc(mod_ready, 1)
                dve.scalar_tensor_tensor(shift_scale[layer][:, 1], ps[:, 1], 1.0,
                                         bias_cols[:, r + KD:r + 2 * KD].rearrange("p (k a) -> p k a", a=1)
                                         .to_broadcast([P, KD, B]), ALU.add, ALU.add).then_inc(mod_ready, 1)

            dve.wait_ge(bias_transposed, 1)
            dve.tensor_copy(bias_cols[:, :], ps_bias[:, 0, 0:ROWS]).then_inc(bias_ready, 1)
            dve.wait_ge(x_first_loaded, 16)
            ln_stats(0, 0)
            split_weight(w_up_hi[0], w_up[0], w_up_loaded[0], w_up_hi_ready[0])
            ln_apply(0, 0, first=True)
            dve.wait_ge(bias_ready, 1)
            modulation(0)
            split_norm(0, first=True)
            dve.wait_ge(x_rest_loaded, 16 * (NG - 1))
            ln_stats(0, 1)
            ln_apply(0, 1)
            split_weight(w_down_hi[0], w_down[0], w_down_loaded[0], w_down_hi_ready[0])
            dve.wait_ge(mod_summed, 3)
            dve.wait_ge(gate_bias_loaded, 16)
            dve.tensor_tensor(gate_rows[:, :, :], ps_gate[0:B, :, :], gate_bias[:, :, :], ALU.add
                              ).then_inc(gates_ready, 1)
            modulation(1)

            split_norm(1)
            split_h(0, 0, 0, first=True)
            ln_stats(0, 2)
            split_h(0, 0, 1, first=True)
            ln_apply(0, 2)
            split_weight(w_up_hi[1], w_up[1], w_up_loaded[1], w_up_hi_ready[1])
            dve.wait_ge(down_bias_loaded, 32)

            def step(split, h_split, down, ln, i, first_down=False):
                split_norm(i)
                split_h(h_split, i - 1, 0)
                add_bias(down, i - 2, 0, first_down)
                if ln is not None:
                    ln_stats(ln, i + 1)
                split_h(h_split, i - 1, 1)
                add_bias(down, i - 2, 1, first_down)
                if ln is not None:
                    ln_apply(ln, i + 1)

            step(0, 0, 0, 0, 2, first_down=True)
            split_weight(w_down_hi[1], w_down[1], w_down_loaded[1], w_down_hi_ready[1])
            step(0, 0, 0, 1, 3)
            step(1, 0, 0, 1, 4)
            step(1, 1, 0, 1, 5)
            step(1, 1, 1, 1, 6)
            step(1, 1, 1, None, 7)
            for hb in range(HALVES):
                split_h(1, LAST, hb)
                add_bias(1, LAST - 1, hb)
            for hb in range(HALVES):
                add_bias(1, LAST, hb)

        @block.gpsimd
        def _(pool):
            pool.memset(ident[:, :], 0.0).then_inc(ident_zeroed, 1)
            pool.wait_ge(ident_zeroed, 1)
            pool.affine_select(out=ident[:, :], in_=ident[:, :], compare_op=ALU.not_equal, fill=1.0, base=0,
                               pattern=[[-1, P]], channel_multiplier=1).then_inc(ident_ready, 1)
            pool.memset(minus_half[:, :], -0.5).then_inc(constants_ready, 1)

            def inverse_std(i):
                pool.wait_ge(vareps_done, i + 1)
                pool.tensor_tensor(rstd[:, :], vareps[:, :], minus_half[:, :], ALU.pow).then_inc(rstd_done, 1)

            def split_norm(i):
                for k in range(KD):
                    pool.wait_ge(norm_hi_ready, KD * i + k + 1)
                    pool.tensor_tensor(norm_lo[:, k, :], norm[:, k, :], norm_hi[:, k, :].bitcast(F32),
                                       ALU.subtract).then_inc(norm_lo_ready, 1)

            def split_h(layer, i, hb):
                cols = slice(HT * hb, HT * (hb + 1))
                for q in range(M[layer] // 2):
                    pool.wait_ge(h_hi_ready[q], HALVES * runs(2 * q, i) + hb + 1)
                    pool.tensor_tensor(h_lo[:, 2 * q:2 * q + 2, cols], h[:, 2 * q:2 * q + 2, cols],
                                       h_hi[:, 2 * q:2 * q + 2, cols].bitcast(F32),
                                       ALU.subtract).then_inc(h_lo_ready[q], 1)

            def add_residual(layer, i, hb):
                g = group(layer, i)
                pool.wait_ge(biased, HALVES * i + hb + 1)
                pool.tensor_tensor(branch[:, hb, :, :], branch[:, hb, :, :],
                                   gate[layer][:, bass.ds(HALVES * g + hb, 1), :].to_broadcast([P, CT, D]),
                                   ALU.mult).then_inc(gated, 1)
                pool.wait_ge(gated, HALVES * i + hb + 1)
                dst = xres[:, bass.ds(g, 1), CT * hb:CT * (hb + 1), :].rearrange("p a c f -> p (a c) f")
                pool.tensor_tensor(dst, dst, branch[:, hb, :, :], ALU.add).then_inc(residual_done, 1)

            def split_weight(dst, src, hi, hi_ready, ready):
                pool.wait_ge(hi_ready, 1)
                pool.tensor_tensor(dst[:, :, :], src[:, :, :], hi[:, :, :].bitcast(F32),
                                   ALU.subtract).then_inc(ready, 1)

            pool.wait_ge(constants_ready, 1)
            inverse_std(0)
            split_weight(w_up_lo[0], w_up[0], w_up_hi[0], w_up_hi_ready[0], w_up_lo_ready[0])
            split_norm(0)
            inverse_std(1)
            split_weight(w_down_lo[0], w_down[0], w_down_hi[0], w_down_hi_ready[0], w_down_lo_ready[0])
            split_norm(1)
            split_h(0, 0, 0)
            inverse_std(2)
            split_h(0, 0, 1)
            split_weight(w_up_lo[1], w_up[1], w_up_hi[1], w_up_hi_ready[1], w_up_lo_ready[1])
            pool.wait_ge(gates_loaded[0], 16)

            def step(h_split, down, ln, i):
                split_norm(i)
                split_h(h_split, i - 1, 0)
                add_residual(down, i - 2, 0)
                if ln:
                    inverse_std(i + 1)
                split_h(h_split, i - 1, 1)
                add_residual(down, i - 2, 1)

            step(0, 0, True, 2)
            split_weight(w_down_lo[1], w_down[1], w_down_hi[1], w_down_hi_ready[1], w_down_lo_ready[1])
            step(0, 0, True, 3)
            step(0, 0, True, 4)
            step(1, 0, True, 5)
            pool.wait_ge(gates_loaded[1], 16)
            step(1, 1, True, 6)
            step(1, 1, False, 7)
            for hb in range(HALVES):
                split_h(1, LAST, hb)
                add_residual(1, LAST - 1, hb)
            for hb in range(HALVES):
                add_residual(1, LAST, hb)

        @block.tensor
        def _(pe):
            def transpose_xhat(i, first=False):
                for k in range(KD):
                    if not first:
                        pe.wait_ge(norm_ready, HALVES * (KD * (i - 1) + k + 1))
                    for t in range(TILES):
                        if k == 0:
                            pe.wait_ge(xhat_ready, TILES * i + t + 1)
                        mm = pe.transpose(ps_tr[k][:, P * t:P * (t + 1)], xhat[:, t, P * k:P * (k + 1)], ident[:, :])
                    mm.then_inc(transposed, 1)

            def up(layer, i, first):
                for m in range(M[layer]):
                    cols = slice(P * m, P * (m + 1))
                    if not first[m]:
                        pe.wait_ge(gelu_done[m], runs(m, i))
                    for k in range(KD):
                        if m == 0:
                            pe.wait_ge(norm_hi_ready, KD * i + k + 1)
                        pe.matmul(ps_up[m][:, :], w_up_lo[layer][:, k, cols], norm_hi[:, k, :],
                                  start=(k == 0), stop=False)
                        pe.matmul(ps_up[m][:, :], w_up_hi[layer][:, k, cols], norm_hi[:, k, :],
                                  start=False, stop=False)
                        if m == 0:
                            pe.wait_ge(norm_lo_ready, KD * i + k + 1)
                        mm = pe.matmul(ps_up[m][:, :], w_up_hi[layer][:, k, cols], norm_lo[:, k, :],
                                       start=False, stop=(k == KD - 1))
                    mm.then_inc(up_done[m], 1)

            def down(layer, i, first=False):
                for hb in range(HALVES):
                    if not first:
                        pe.wait_ge(biased, HALVES * (i - 1) + hb + 1)
                    for c in range(CT):
                        rows = slice(P * (CT * hb + c), P * (CT * hb + c + 1))
                        for m in range(M[layer]):
                            if c == 0 and m % 2 == 0:
                                pe.wait_ge(h_lo_ready[m // 2], HALVES * runs(m, i) + hb + 1)
                            pe.matmul(ps_down[hb][:, c, :], h_hi[:, m, rows], w_down_hi[layer][:, m, :],
                                      start=(m == 0), stop=False)
                            pe.matmul(ps_down[hb][:, c, :], h_hi[:, m, rows], w_down_lo[layer][:, m, :],
                                      start=False, stop=False)
                            mm = pe.matmul(ps_down[hb][:, c, :], h_lo[:, m, rows], w_down_hi[layer][:, m, :],
                                           start=False, stop=(m == M[layer] - 1))
                    mm.then_inc(down_done, 1)

            def modulation(layer):
                for s in range(2):
                    for j in range(KD):
                        for k in range(KD):
                            mm = pe.matmul(ps_mod[layer][:, (s * KD + j) * B:(s * KD + j + 1) * B],
                                           ada_sb[:, k, layer, D * s + P * j:D * s + P * (j + 1)],
                                           cond_silu[:, k, :], start=(k == 0), stop=(k == KD - 1))
                mm.then_inc(mod_summed, 1)

            pe.wait_ge(ident_ready, 1)
            pe.wait_ge(cond_loaded, 16)
            for k in range(KD):
                mm = pe.transpose(ps_cond[:, 0, B * k:B * (k + 1)], cond_rows[:, P * k:P * (k + 1)], ident[0:B, 0:B])
            mm.then_inc(cond_transposed, 1)
            pe.wait_ge(biases_loaded, 48)
            pe.transpose(ps_bias[:, 0, 0:ROWS], bias_rows[:, :], ident[0:ROWS, 0:ROWS]).then_inc(bias_transposed, 1)
            pe.wait_ge(silu_ready, 1)
            pe.wait_ge(ada_loaded[0], 16)
            modulation(0)
            transpose_xhat(0, first=True)
            pe.wait_ge(w_up_hi_ready[0], 1)
            pe.wait_ge(w_up_lo_ready[0], 1)
            up(0, 0, [True] * MMAX)
            transpose_xhat(1)
            pe.wait_ge(ada_loaded[1], 16)
            modulation(1)
            for k in range(KD):
                mm = pe.matmul(ps_gate[0:B, :, :], cond_silu[:, k, :], ada_sb[:, k, :, 2 * D:3 * D],
                               start=(k == 0), stop=(k == KD - 1))
            mm.then_inc(mod_summed, 1)
            up(0, 1, [False] * MMAX)

            pe.wait_ge(w_down_hi_ready[0], 1)
            pe.wait_ge(w_down_lo_ready[0], 1)
            pe.wait_ge(gates_ready, 1)
            transpose_xhat(2)
            down(0, 0, first=True)
            up(0, 2, [False] * MMAX)
            transpose_xhat(3)
            down(0, 1)
            up(0, 3, [False] * MMAX)
            pe.wait_ge(w_up_hi_ready[1], 1)
            pe.wait_ge(w_up_lo_ready[1], 1)
            pe.wait_ge(mod_ready, 4)
            transpose_xhat(4)
            down(0, 2)
            up(1, 4, [False] * M[0] + [True] * (MMAX - M[0]))
            transpose_xhat(5)
            down(0, 3)
            up(1, 5, [False] * MMAX)
            pe.wait_ge(w_down_hi_ready[1], 1)
            pe.wait_ge(w_down_lo_ready[1], 1)
            with pe.Fori(NG + 2, LAST + 1) as i:
                transpose_xhat(i)
                down(1, i - 2)
                up(1, i, [False] * MMAX)
            down(1, LAST - 1)
            down(1, LAST)


_INS = ['x', 'cond_1024', 'L0_cond_ada_w', 'L0_cond_ada_b', 'L0_cond_ssm_w1', 'L0_cond_ssm_b1', 'L0_cond_ssm_w2',
        'L0_cond_ssm_b2', 'L0_cond_ff_w1', 'L0_cond_ff_b1', 'L0_cond_ff_w2', 'L0_cond_ff_b2']


def kernel(**inputs):
    import numpy as _np
    import concourse.bacc as _bacc
    from concourse import mybir as _mybir
    from concourse.bass_utils import run_bass_kernel_spmd as _run

    nc = _bacc.Bacc("TRN2", target_bir_lowering=False, num_devices=1)
    arrays, args = {}, []
    for name in _INS:
        a = _np.ascontiguousarray(inputs[name])
        arrays[f"in_{name}_dram"] = a
        args.append(nc.dram_tensor(f"in_{name}_dram", a.shape, _mybir.dt.from_np(a.dtype), kind="ExternalInput").ap())
    B, _, D = arrays["in_x_dram"].shape
    args.append(nc.dram_tensor("gate_scratch", (B, 2, D), _mybir.dt.float32, kind="Internal").ap())
    args.append(nc.dram_tensor("out_0_dram", arrays["in_x_dram"].shape, _mybir.dt.float32, kind="ExternalOutput").ap())
    conditioned_block_kernel(nc, *args)
    r = _run(nc, [arrays], core_ids=[0])
    return r.results[0]["out_0_dram"]
```

```python
from contextlib import ExitStack

import concourse.bass as bass
from concourse import mybir

ALU = mybir.AluOpType
ACT = mybir.ActivationFunctionType
F32 = mybir.dt.float32
F32R = mybir.dt.float32r

P = 128
EPS = 1e-6
HALVES = 2


def conditioned_block_kernel(
    nc: bass.Bass,
    x: bass.AP,
    cond: bass.AP,
    ada_w: bass.AP,
    ada_b: bass.AP,
    w1: bass.AP,
    b1: bass.AP,
    w2: bass.AP,
    b2: bass.AP,
    ff_w1: bass.AP,
    ff_b1: bass.AP,
    ff_w2: bass.AP,
    ff_b2: bass.AP,
    gate_scratch: bass.AP,
    out: bass.AP,
):
    B, S, D = x.shape
    KD = D // P
    CT = S // P
    NG = B // HALVES
    TILES = HALVES * CT
    GT = TILES * P
    HT = CT * P
    HIDDEN = (w1.shape[1], ff_w1.shape[1])
    M = tuple(h // P for h in HIDDEN)
    MMAX = max(M)
    LAST = 2 * NG - 1
    assert (S, D, GT, HIDDEN) == (256, 256, 512, (256, 512))

    NB_ADA = ada_b.shape[0] // P
    ROW_B1 = (NB_ADA, NB_ADA + M[0])
    ROWS = NB_ADA + M[0] + M[1]
    SHIFT, SCALE, GATE = range(3)

    with ExitStack() as ctx:
        def sb(name, shape, dt=F32):
            return ctx.enter_context(nc.sbuf_tensor(name, shape, dt))

        def psum(name, shape):
            return ctx.enter_context(nc.psum_tensor(name, shape, F32))

        def sem(name):
            return ctx.enter_context(nc.semaphore(name))

        xres = sb("xres", [P, NG, TILES, D])
        xhat = sb("xhat", [P, TILES, D])
        stats = sb("stats", [P, NG + 1, TILES, 6])
        meanvar = sb("meanvar", [P, NG + 1, TILES, 2])
        vareps = sb("vareps", [P, NG + 1, TILES])
        rstd = sb("rstd", [P, NG + 1, TILES])
        mean_rstd = sb("mean_rstd", [P, NG + 1, TILES])
        minus_half = sb("minus_half", [P, TILES])
        ident = sb("ident", [P, P])

        norm_hi = sb("norm_hi", [P, NG, KD, GT], F32R)
        norm_lo = sb("norm_lo", [P, NG, KD, GT], F32R)
        h = sb("h", [P, MMAX, GT])
        h_hi = sb("h_hi", [P, MMAX, GT], F32R)
        h_lo = sb("h_lo", [P, MMAX, GT], F32R)
        branch = sb("branch", [P, HALVES, CT, D])
        gated_bias = sb("gated_bias", [P, HALVES, D])

        w_up = [sb(f"w_up{n}", [P, KD, HIDDEN[n]]) for n in range(2)]
        w_up_hi = [sb(f"w_up_hi{n}", [P, KD, HIDDEN[n]], F32R) for n in range(2)]
        w_up_lo = [sb(f"w_up_lo{n}", [P, KD, HIDDEN[n]], F32R) for n in range(2)]
        w_down = [sb(f"w_down{n}", [P, M[n], D]) for n in range(2)]
        w_down_hi = [sb(f"w_down_hi{n}", [P, M[n], D], F32R) for n in range(2)]
        w_down_lo = [sb(f"w_down_lo{n}", [P, M[n], D], F32R) for n in range(2)]

        cond_rows = sb("cond_rows", [B, D])
        cond_silu = sb("cond_silu", [P, KD, B])
        ada_sb = sb("ada_sb", [P, 2, 3, KD, D])
        bias_rows = sb("bias_rows", [ROWS, P])
        bias_cols = sb("bias_cols", [P, ROWS])
        shift = sb("shift", [P, KD, 2, B])
        scale = sb("scale", [P, KD, 2 * B])
        up_bias = [sb(f"up_bias{n}", [P, M[n], B]) for n in range(2)]
        gate_bias = sb("gate_bias", [B, 2, D])
        gate_rows = sb("gate_rows", [B, 2, D])
        gate = sb("gate", [P, 2 * B, D])
        down_bias = [sb(f"down_bias{n}", [P, D]) for n in range(2)]
        warm = sb("warm", [P, 3])
        zeros = sb("zeros", [P, GT], mybir.dt.bfloat16)

        ps_tr = [psum(f"ps_tr{k}", [P, GT]) for k in range(KD)]
        ps_up = [psum(f"ps_up{m}", [P, GT]) for m in range(MMAX)]
        ps_down = [psum(f"ps_down{hb}", [P, CT, D]) for hb in range(HALVES)]
        ps_last = [bank[:, 0:D] for bank in (ps_up[0], ps_up[1], ps_tr[0], ps_tr[1])]
        ps_cond = ps_down[0][:, 0, 0:KD * B]
        ps_bias = ps_down[1][:, 0, 0:ROWS]
        ps_scale = [ps_down[0][:, 0, 64:64 + KD * B], ps_up[3][:, 0:KD * B]]
        ps_shift = [ps_down[1][:, 0, 64:64 + KD * B], ps_up[3][:, 64:64 + KD * B]]
        ps_up_bias = [ps_down[0][:, 1, 0:M[0] * B], ps_up[3][:, 128:128 + M[1] * B]]
        ps_gate = [ps_up[2][0:B, D * n:D * (n + 1)] for n in range(2)]

        cond_loaded = sem("cond_loaded")
        biases_loaded = [sem(f"biases_loaded{n}") for n in range(3)]
        gate_bias_loaded = sem("gate_bias_loaded")
        ada_loaded = [[sem(f"ada_loaded{n}_{s}") for s in range(3)] for n in range(2)]
        x_first_loaded = [sem(f"x_first_loaded{hb}") for hb in range(HALVES)]
        x_loaded = [sem(f"x_loaded{g}") for g in range(NG)]
        w_up_loaded = [sem(f"w_up_loaded{n}") for n in range(2)]
        w_down_loaded = [sem(f"w_down_loaded{n}") for n in range(2)]
        down_bias_loaded = sem("down_bias_loaded")
        gates_stored = [sem(f"gates_stored{n}") for n in range(2)]
        gates_loaded = [sem(f"gates_loaded{n}") for n in range(2)]
        out_stored = sem("out_stored")

        zeros_ready = sem("zeros_ready")
        ident_zeroed = sem("ident_zeroed")
        ident_ready = sem("ident_ready")
        constants_ready = sem("constants_ready")
        cond_transposed = sem("cond_transposed")
        bias_transposed = sem("bias_transposed")
        silu_ready = sem("silu_ready")
        bias_ready = sem("bias_ready")
        scale_summed = sem("scale_summed")
        shift_summed = sem("shift_summed")
        gate_summed = sem("gate_summed")
        up_bias_summed = sem("up_bias_summed")
        scale_ready = sem("scale_ready")
        shift_ready = sem("shift_ready")
        up_bias_ready = sem("up_bias_ready")
        gates_ready = sem("gates_ready")

        stats_done = sem("stats_done")
        meanvar_done = sem("meanvar_done")
        vareps_done = sem("vareps_done")
        rstd_done = sem("rstd_done")
        mean_rstd_done = sem("mean_rstd_done")
        xhat_ready = sem("xhat_ready")
        transposed = sem("transposed")
        norm_hi_ready = sem("norm_hi_ready")
        norm_lo_ready = sem("norm_lo_ready")
        up_done = [sem(f"up_done{m}") for m in range(MMAX)]
        gelu_done = [sem(f"gelu_done{m}") for m in range(MMAX)]
        h_hi_ready = [sem(f"h_hi_ready{q}") for q in range(MMAX // 2)]
        h_lo_ready = [sem(f"h_lo_ready{q}") for q in range(MMAX // 2)]
        down_done = sem("down_done")
        biased = sem("biased")
        gated = sem("gated")
        residual_done = sem("residual_done")
        bias_gated = sem("bias_gated")
        last_down_done = sem("last_down_done")
        last_gated = sem("last_gated")
        last_residual = sem("last_residual")
        w_up_hi_ready = [sem(f"w_up_hi_ready{n}") for n in range(2)]
        w_up_lo_ready = [sem(f"w_up_lo_ready{n}") for n in range(2)]
        w_down_hi_ready = [sem(f"w_down_hi_ready{n}") for n in range(2)]
        w_down_lo_ready = [sem(f"w_down_lo_ready{n}") for n in range(2)]

        def slot(layer, i):
            return NG if layer else i

        def runs(m, i):
            return i if m < M[0] else i - NG

        def pair_ready(m):
            return h_lo_ready[m // 2]

        block = ctx.enter_context(nc.Block())

        ada_v = ada_w.rearrange("(k p) (l s n) -> p l s k n", p=P, l=2, s=3)

        def load_ada(eng, n, s):
            eng.dma_start(ada_sb[:, n, s], ada_v[:, n, s]).then_inc(ada_loaded[n][s], 16)

        def load_x(eng, b, signal):
            g, hb = b // HALVES, b % HALVES
            eng.dma_start(xres[:, g, CT * hb:CT * (hb + 1), :].rearrange("p c f -> p (c f)"),
                          x[b].rearrange("(p c) f -> p (c f)", c=CT)).then_inc(signal, 16)

        def load_group(eng, g, signal):
            eng.dma_start(xres[:, g].rearrange("p (b c) f -> p b (c f)", b=HALVES),
                          x[HALVES * g:HALVES * (g + 1)].rearrange("b (p c) f -> p b (c f)", c=CT)
                          ).then_inc(signal, 16)

        def load_w(eng, dst, w, signal):
            eng.dma_start(dst[:, :, :], w.rearrange("(k p) n -> p k n", p=P)).then_inc(signal, 16)

        @block.sync
        def _(sp):
            sp.dma_start(cond_rows[:, :], cond).then_inc(cond_loaded, 16)
            load_x(sp, 1, x_first_loaded[1])
            load_group(sp, 1, x_loaded[1])
            load_w(sp, w_up[0], w1, w_up_loaded[0])
            load_ada(sp, 0, SHIFT)
            load_ada(sp, 0, GATE)
            load_w(sp, w_down[0], w2, w_down_loaded[0])
            load_group(sp, 2, x_loaded[2])
            load_group(sp, 3, x_loaded[3])
            for part in (SCALE, SHIFT, GATE):
                load_ada(sp, 1, part)
            load_w(sp, w_up[1], ff_w1, w_up_loaded[1])
            load_w(sp, w_down[1], ff_w2, w_down_loaded[1])

            for n in range(2):
                sp.wait_ge(gates_ready, n + 1)
                sp.dma_start(gate_scratch[:, n, :], gate_rows[:, n, :]).then_inc(gates_stored[n], 16)
                sp.wait_ge(gates_stored[n], 16)
                sp.dma_start(gate[:, B * n:B * (n + 1), :],
                             gate_scratch[:, n, :].rearrange("(a b) f -> a b f", a=1).to_broadcast([P, B, D])
                             ).then_inc(gates_loaded[n], 16)

            for i in range(NG, LAST):
                for hb in range(HALVES):
                    b = HALVES * (i - NG) + hb
                    sp.wait_ge(residual_done, HALVES * i + hb + 1)
                    sp.dma_start(out[b].rearrange("(p c) f -> p (c f)", c=CT),
                                 xres[:, i - NG, CT * hb:CT * (hb + 1), :].rearrange("p c f -> p (c f)")
                                 ).then_inc(out_stored, 16)
            for t in range(TILES):
                hb, c = t // CT, t % CT
                sp.wait_ge(last_residual, t + 1)
                sp.dma_start(out[HALVES * (NG - 1) + hb].rearrange("(p c) f -> p c f", c=CT)[:, c, :],
                             xres[:, NG - 1, t, :]).then_inc(out_stored, 16)
            sp.wait_ge(out_stored, 16 * (HALVES * (NG - 1) + TILES))

        @block.scalar
        def _(act):
            load_x(act, 0, x_first_loaded[0])
            load_ada(act, 0, SCALE)
            act.dma_start(bias_rows[0:NB_ADA, :], ada_b.rearrange("(r p) -> r p", p=P)).then_inc(biases_loaded[0], 16)
            act.wait_ge(constants_ready, 1)
            act.activation(warm[:, 0:1], minus_half[:, 0:1], ACT.Silu)
            act.wait_ge(cond_transposed, 1)
            act.activation(cond_silu[:, :, :].rearrange("p k b -> p (k b)"), ps_cond, ACT.Silu).then_inc(silu_ready, 1)
            act.activation(warm[:, 1:2], minus_half[:, 0:1], ACT.Gelu)

            def split_weight(dst, src, loaded, ready):
                act.wait_ge(loaded, 16)
                act.activation(dst[:, :, :], src[:, :, :], ACT.Identity).then_inc(ready, 1)

            def normalise(layer, i):
                g, n = i - NG * layer, slot(layer, i)
                act.wait_ge(mean_rstd_done, 1)
                act.wait_ge(transposed, KD * i)
                for t in range(TILES):
                    act.activation(xhat[:, t, :], xres[:, bass.ds(g, 1), t, :].rearrange("p a f -> p (a f)"),
                                   ACT.Identity, bias=mean_rstd[:, n, t:t + 1], scale=rstd[:, n, t:t + 1]
                                   ).then_inc(xhat_ready, 1)

            def split_norm(i, reused):
                g = i - NG * reused
                for k in range(KD):
                    act.wait_ge(transposed, KD * i + k + 1)
                    if reused:
                        act.wait_ge(up_done[M[0] - 1], i - NG + 1)
                    for hb in range(HALVES):
                        cols = slice(HT * hb, HT * (hb + 1))
                        act.activation(norm_hi[:, bass.ds(g, 1), k, cols].rearrange("p a n -> p (a n)"),
                                       ps_tr[k][:, cols], ACT.Identity,
                                       scale=scale[:, k, bass.ds(HALVES * i + hb, 1)]).then_inc(norm_hi_ready, 1)

            def gelu(layer, i, chunks, first):
                func = (ACT.Gelu, ACT.Gelu_apprx_tanh)[layer]
                for m in chunks:
                    act.wait_ge(up_done[m], runs(m, i) + 1)
                    if not first:
                        act.wait_ge(pair_ready(m), HALVES * runs(m, i))
                    for hb in range(HALVES):
                        cols = slice(HT * hb, HT * (hb + 1))
                        b = HALVES * (i - NG * layer) + hb
                        act.activation(h[:, m, cols], ps_up[m][:, cols], func,
                                       bias=up_bias[layer][:, m, bass.ds(b, 1)]).then_inc(gelu_done[m], 1)

            def split_h(layer, i, hb, m, first=False):
                cols = slice(HT * hb, HT * (hb + 1))
                if not first:
                    act.wait_ge(down_done, HALVES * (i - 1) + hb + 1)
                act.wait_ge(gelu_done[m + 1], HALVES * (runs(m, i) + 1))
                act.activation(h_hi[:, m:m + 2, cols], h[:, m:m + 2, cols], ACT.Identity
                               ).then_inc(h_hi_ready[m // 2], 1)

            def narrow_step(i, first=False, norm_reused=False):
                gelu(0, i, [0], first)
                split_norm(i + 1, norm_reused)
                gelu(0, i, [1], first)
                for hb in range(HALVES):
                    split_h(0, i, hb, 0, first)

            def wide_step(i, last=False):
                first = isinstance(i, int) and i == NG
                gelu(1, i, [0], False)
                if not last:
                    split_norm(i + 1, True)
                gelu(1, i, [1], False)
                split_h(1, i, 0, 0)
                gelu(1, i, [2, 3], first)
                split_h(1, i, 0, 2)
                split_h(1, i, 1, 0)
                split_h(1, i, 1, 2)

            split_weight(w_up_hi[0], w_up[0], w_up_loaded[0], w_up_hi_ready[0])
            act.wait_ge(scale_ready, 1)
            split_norm(0, False)
            normalise(0, 1)
            act.wait_ge(up_bias_ready, 1)
            gelu(0, 0, [0, 1], True)
            split_weight(w_down_hi[0], w_down[0], w_down_loaded[0], w_down_hi_ready[0])
            split_norm(1, False)
            for hb in range(HALVES):
                split_h(0, 0, hb, 0, True)
            split_weight(w_up_hi[1], w_up[1], w_up_loaded[1], w_up_hi_ready[1])
            narrow_step(1)
            split_weight(w_down_hi[1], w_down[1], w_down_loaded[1], w_down_hi_ready[1])
            narrow_step(2)
            act.wait_ge(scale_ready, 2)
            narrow_step(3, norm_reused=True)
            act.wait_ge(up_bias_ready, 2)
            act.activation(warm[:, 2:3], minus_half[:, 0:1], ACT.Gelu_apprx_tanh)
            wide_step(NG)
            with act.Fori(NG + 1, LAST) as i:
                wide_step(i)
            wide_step(LAST, last=True)

        @block.vector
        def _(dve):
            def ln_sums(layer, i):
                g, n = i - NG * layer, slot(layer, i)
                if layer == 1:
                    dve.wait_ge(residual_done, HALVES * (g + 1))
                for t in range(TILES):
                    if i == 0 and layer == 0:
                        dve.wait_ge(x_first_loaded[t // CT], 16)
                    elif layer == 0 and t == 0:
                        dve.wait_ge(x_loaded[i], 16)
                    dve.bn_stats(stats[:, n, t, :], xres[:, bass.ds(g, 1), t, :].rearrange("p a f -> p (a f)")
                                 ).then_inc(stats_done, 1)

            def ln_variance(layer, i):
                n = slot(layer, i)
                for t in range(TILES):
                    dve.wait_ge(stats_done, TILES * i + t + 1)
                    dve.bn_aggr(meanvar[:, n, t, :], stats[:, n, t, :]).then_inc(meanvar_done, 1)
                dve.wait_ge(meanvar_done, TILES * (i + 1))
                dve.tensor_scalar(vareps[:, n, :], meanvar[:, n, :, 1], EPS, None, ALU.add).then_inc(vareps_done, 1)

            def ln_stats(layer, i):
                ln_sums(layer, i)
                ln_variance(layer, i)

            def ln_offset(i):
                dve.wait_ge(rstd_done, i + 1)
                dve.scalar_tensor_tensor(mean_rstd[:, i, :], meanvar[:, i, :, 0], -1.0, rstd[:, i, :],
                                         ALU.mult, ALU.mult).then_inc(mean_rstd_done, 1)

            def normalise(layer, i):
                g, n = i - NG * layer, slot(layer, i)
                dve.wait_ge(rstd_done, i + 1)
                if not (layer == 0 and i == 0):
                    dve.wait_ge(transposed, KD * i)
                for t in range(TILES):
                    dve.tensor_scalar(xhat[:, t, :], xres[:, bass.ds(g, 1), t, :].rearrange("p a f -> p (a f)"),
                                      meanvar[:, n, t, 0:1], rstd[:, n, t:t + 1],
                                      ALU.subtract, ALU.mult).then_inc(xhat_ready, 1)

            def split_norm(i, reused):
                g = i - NG * reused
                for k in range(KD):
                    dve.wait_ge(norm_hi_ready, HALVES * (KD * i + k + 1))
                    for hb in range(HALVES):
                        cols = slice(HT * hb, HT * (hb + 1))
                        dve.scalar_tensor_tensor(
                            norm_lo[:, bass.ds(g, 1), k, cols].rearrange("p a n -> p (a n)"), ps_tr[k][:, cols],
                            scale[:, k, bass.ds(HALVES * i + hb, 1)],
                            norm_hi[:, bass.ds(g, 1), k, cols].rearrange("p a n -> p (a n)").bitcast(F32),
                            ALU.mult, ALU.subtract).then_inc(norm_lo_ready, 1)

            def split_h(layer, i, hb):
                cols = slice(HT * hb, HT * (hb + 1))
                for m in range(0, M[layer], 2):
                    dve.wait_ge(h_hi_ready[m // 2], HALVES * runs(m, i) + hb + 1)
                    dve.tensor_tensor(h_lo[:, m:m + 2, cols], h[:, m:m + 2, cols],
                                      h_hi[:, m:m + 2, cols].bitcast(F32), ALU.subtract
                                      ).then_inc(h_lo_ready[m // 2], 1)

            def add_bias(layer, i, hb, first=False):
                dve.wait_ge(down_done, HALVES * i + hb + 1)
                if not first:
                    dve.wait_ge(residual_done, HALVES * (i - 1) + hb + 1)
                dve.tensor_tensor(branch[:, hb, :, :], ps_down[hb][:, :, :],
                                  down_bias[layer][:, :].rearrange("p (a f) -> p a f", a=1).to_broadcast([P, CT, D]),
                                  ALU.add).then_inc(biased, 1)

            def bias_of(row, chunks):
                return bias_cols[:, row:row + chunks].rearrange("p (k a) -> p k a", a=1).to_broadcast([P, chunks, B])

            def chunked(ps):
                return ps.rearrange("p (k b) -> p k b", b=B)

            def scale_of(n):
                dve.wait_ge(scale_summed, n + 1)
                if n == 1:
                    dve.wait_ge(shift_summed, 2)
                dve.scalar_tensor_tensor(scale[:, :, B * n:B * (n + 1)], chunked(ps_scale[n]), 1.0,
                                         bias_of(KD * (3 * n + SCALE), KD), ALU.add, ALU.add).then_inc(scale_ready, 1)

            def shift_of(n):
                dve.wait_ge(shift_summed, n + 1)
                dve.tensor_tensor(shift[:, :, n, :], chunked(ps_shift[n]),
                                  bias_of(KD * (3 * n + SHIFT), KD), ALU.add).then_inc(shift_ready, 1)

            def up_bias_of(n):
                dve.wait_ge(up_bias_summed, n + 1)
                dve.tensor_tensor(up_bias[n][:, :, :], chunked(ps_up_bias[n]), bias_of(ROW_B1[n], M[n]),
                                  ALU.add).then_inc(up_bias_ready, 1)

            def gate_of(n):
                dve.wait_ge(gate_summed, n + 1)
                dve.tensor_tensor(gate_rows[:, n, :], ps_gate[n], gate_bias[:, n, :], ALU.add).then_inc(gates_ready, 1)

            ln_stats(0, 0)
            ln_sums(0, 1)
            normalise(0, 0)
            dve.wait_ge(bias_transposed, 1)
            dve.tensor_copy(bias_cols[:, :], ps_bias).then_inc(bias_ready, 1)
            dve.wait_ge(bias_ready, 1)
            scale_of(0)
            ln_variance(0, 1)
            shift_of(0)
            split_norm(0, False)
            ln_offset(1)
            up_bias_of(0)
            dve.wait_ge(gate_bias_loaded, 16)
            gate_of(0)
            ln_stats(0, 2)
            split_norm(1, False)
            normalise(0, 2)
            scale_of(1)
            shift_of(1)
            gate_of(1)
            ln_stats(0, 3)
            dve.wait_ge(down_bias_loaded, 32)
            split_norm(2, False)
            normalise(0, 3)
            add_bias(0, 0, 0, True)
            split_h(0, 1, 0)
            add_bias(0, 0, 1, True)
            split_h(0, 1, 1)
            up_bias_of(1)

            def step(layer, i, down, ln=True, norm_reused=True, last=False):
                if not last:
                    split_norm(i + 1, norm_reused)
                if ln:
                    ln_stats(1, i + 2)
                add_bias(down, i - 1, 0)
                if ln:
                    normalise(1, i + 2)
                split_h(layer, i, 0)
                add_bias(down, i - 1, 1)
                split_h(layer, i, 1)

            step(0, 2, 0, norm_reused=False)
            step(0, 3, 0)
            step(1, 4, 0)
            step(1, 5, 1)
            step(1, 6, 1, ln=False)
            step(1, 7, 1, ln=False, last=True)
            dve.wait_ge(residual_done, HALVES * LAST)
            dve.wait_ge(bias_gated, 2 * HALVES)
            for t in range(TILES):
                hb, c = t // CT, t % CT
                dve.wait_ge(last_down_done, t + 1)
                dve.tensor_tensor(branch[:, hb, c, :], ps_last[t], gate[:, HALVES * LAST + hb, :], ALU.mult
                                  ).then_inc(last_gated, 1)
                dve.wait_ge(last_gated, t + 1)
                dve.tensor_tensor(xres[:, NG - 1, t, :], xres[:, NG - 1, t, :], branch[:, hb, c, :], ALU.add
                                  ).then_inc(last_residual, 1)

        @block.gpsimd
        def _(pool):
            pool.memset(minus_half[:, :], -0.5).then_inc(constants_ready, 1)
            pool.memset(ident[:, :], 0.0).then_inc(ident_zeroed, 1)
            pool.wait_ge(ident_zeroed, 1)
            pool.affine_select(out=ident[:, :], in_=ident[:, :], compare_op=ALU.not_equal, fill=1.0, base=0,
                               pattern=[[-1, P]], channel_multiplier=1).then_inc(ident_ready, 1)
            pool.memset(zeros[:, :], 0.0).then_inc(zeros_ready, 1)
            for n, b in enumerate((b1, ff_b1)):
                pool.dma_start(bias_rows[ROW_B1[n]:ROW_B1[n] + M[n], :], b.rearrange("(r p) -> r p", p=P)
                               ).then_inc(biases_loaded[n + 1], 16)
            pool.dma_start(gate_bias[:, :, :],
                           ada_b.rearrange("(a l n) -> a l n", a=1, l=2)[:, :, 2 * D:3 * D].to_broadcast([B, 2, D])
                           ).then_inc(gate_bias_loaded, 16)

            def inverse_std(layer, i):
                n = slot(layer, i)
                pool.wait_ge(vareps_done, i + 1)
                pool.tensor_tensor(rstd[:, n, :], vareps[:, n, :], minus_half[:, :], ALU.pow).then_inc(rstd_done, 1)

            def add_residual(layer, i, hb):
                g = i - NG * layer
                pool.wait_ge(biased, HALVES * i + hb + 1)
                pool.tensor_tensor(branch[:, hb, :, :], branch[:, hb, :, :],
                                   gate[:, bass.ds(HALVES * i + hb, 1), :].to_broadcast([P, CT, D]),
                                   ALU.mult).then_inc(gated, 1)
                pool.wait_ge(gated, HALVES * i + hb + 1)
                dst = xres[:, bass.ds(g, 1), CT * hb:CT * (hb + 1), :].rearrange("p a c f -> p (a c) f")
                pool.tensor_tensor(dst, dst, branch[:, hb, :, :], ALU.add).then_inc(residual_done, 1)

            def split_weight(dst, src, hi, hi_ready, ready):
                pool.wait_ge(hi_ready, 1)
                pool.tensor_tensor(dst[:, :, :], src[:, :, :], hi[:, :, :].bitcast(F32),
                                   ALU.subtract).then_inc(ready, 1)

            def split_h(i, hb):
                cols = slice(HT * hb, HT * (hb + 1))
                pool.wait_ge(h_hi_ready[0], HALVES * i + hb + 1)
                pool.tensor_tensor(h_lo[:, 0:2, cols], h[:, 0:2, cols], h_hi[:, 0:2, cols].bitcast(F32),
                                   ALU.subtract).then_inc(h_lo_ready[0], 1)

            pool.wait_ge(constants_ready, 1)
            inverse_std(0, 0)
            split_weight(w_up_lo[0], w_up[0], w_up_hi[0], w_up_hi_ready[0], w_up_lo_ready[0])
            inverse_std(0, 1)
            for n, b in enumerate((b2, ff_b2)):
                pool.dma_start(down_bias[n][:, :], b.rearrange("(a f) -> a f", a=1).to_broadcast([P, D])
                               ).then_inc(down_bias_loaded, 16)
            inverse_std(0, 2)
            split_weight(w_down_lo[0], w_down[0], w_down_hi[0], w_down_hi_ready[0], w_down_lo_ready[0])
            split_h(0, 0)
            split_h(0, 1)
            inverse_std(0, 3)
            split_weight(w_up_lo[1], w_up[1], w_up_hi[1], w_up_hi_ready[1], w_up_lo_ready[1])

            def step(i, down, ln=True):
                if ln:
                    inverse_std(1, i + 2)
                add_residual(down, i - 1, 0)
                add_residual(down, i - 1, 1)

            pool.wait_ge(gates_loaded[0], 16)
            step(1, 0, ln=False)
            step(2, 0)
            split_weight(w_down_lo[1], w_down[1], w_down_hi[1], w_down_hi_ready[1], w_down_lo_ready[1])
            step(3, 0)
            step(4, 0)
            pool.wait_ge(gates_loaded[1], 16)
            step(5, 1)
            pool.wait_ge(down_bias_loaded, 32)
            pool.wait_ge(xhat_ready, TILES * (LAST + 1))
            for hb in range(HALVES):
                pool.tensor_tensor(gated_bias[:, hb, :], gate[:, HALVES * LAST + hb, :], down_bias[1][:, :], ALU.mult
                                   ).then_inc(bias_gated, 1)
                pool.wait_ge(bias_gated, 2 * hb + 1)
                dst = xres[:, NG - 1, CT * hb:CT * (hb + 1), :]
                pool.tensor_tensor(dst, dst, gated_bias[:, hb:hb + 1, :].to_broadcast([P, CT, D]), ALU.add
                                   ).then_inc(bias_gated, 1)
            with pool.Fori(LAST - 1, LAST + 1) as i:
                step(i, 1, ln=False)

        @block.tensor
        def _(pe):
            def transpose_xhat(i, first=False):
                for k in range(KD):
                    if not first:
                        pe.wait_ge(norm_lo_ready, HALVES * (KD * (i - 1) + k + 1))
                    for t in range(TILES):
                        if k == 0:
                            pe.wait_ge(xhat_ready, TILES * i + t + 1)
                        mm = pe.transpose(ps_tr[k][:, P * t:P * (t + 1)], xhat[:, t, P * k:P * (k + 1)], ident[:, :])
                    mm.then_inc(transposed, 1)

            def up(layer, i, chunks, first):
                g = i - NG * layer
                for m in chunks:
                    cols = slice(P * m, P * (m + 1))
                    if not first:
                        pe.wait_ge(gelu_done[m], HALVES * runs(m, i))
                    for k in range(KD):
                        hi = norm_hi[:, bass.ds(g, 1), k, :].rearrange("p a n -> p (a n)")
                        lo = norm_lo[:, bass.ds(g, 1), k, :].rearrange("p a n -> p (a n)")
                        if m == 0:
                            pe.wait_ge(norm_hi_ready, HALVES * (KD * i + k + 1))
                        pe.matmul(ps_up[m][:, :], w_up_lo[layer][:, k, cols], hi, start=(k == 0), stop=False)
                        pe.matmul(ps_up[m][:, :], w_up_hi[layer][:, k, cols], hi, start=False, stop=False)
                        if m == 0:
                            pe.wait_ge(norm_lo_ready, HALVES * (KD * i + k + 1))
                        mm = pe.matmul(ps_up[m][:, :], w_up_hi[layer][:, k, cols], lo,
                                       start=False, stop=(k == KD - 1))
                    mm.then_inc(up_done[m], 1)

            def down_tile(layer, i, t, dst):
                hb, rows = t // CT, slice(P * t, P * (t + 1))
                for m in range(M[layer]):
                    if t % CT == 0 and m % 2 == 0:
                        pe.wait_ge(pair_ready(m), HALVES * runs(m, i) + hb + 1)
                    pe.matmul(dst, h_hi[:, m, rows], w_down_hi[layer][:, m, :], start=(m == 0), stop=False)
                    pe.matmul(dst, h_hi[:, m, rows], w_down_lo[layer][:, m, :], start=False, stop=False)
                    mm = pe.matmul(dst, h_lo[:, m, rows], w_down_hi[layer][:, m, :],
                                   start=False, stop=(m == M[layer] - 1))
                return mm

            def down(layer, i, hb, first=False):
                if not first:
                    pe.wait_ge(biased, HALVES * (i - 1) + hb + 1)
                for c in range(CT):
                    mm = down_tile(layer, i, CT * hb + c, ps_down[hb][:, c, :])
                mm.then_inc(down_done, 1)

            def modulation(n, part, dst, signal):
                pe.wait_ge(ada_loaded[n][part], 16)
                for j in range(KD):
                    for k in range(KD):
                        mm = pe.matmul(dst[:, j * B:(j + 1) * B], ada_sb[:, n, part, k, P * j:P * (j + 1)],
                                       cond_silu[:, k, :], start=(k == 0), stop=(k == KD - 1))
                mm.then_inc(signal, 1)

            def gates(n):
                pe.wait_ge(ada_loaded[n][GATE], 16)
                for k in range(KD):
                    mm = pe.matmul(ps_gate[n], cond_silu[:, k, :], ada_sb[:, n, GATE, k, :],
                                   start=(k == 0), stop=(k == KD - 1))
                mm.then_inc(gate_summed, 1)

            def shift_product(n):
                pe.wait_ge(shift_ready, n + 1)
                for m in range(M[n]):
                    for k in range(KD):
                        mm = pe.matmul(ps_up_bias[n][:, m * B:(m + 1) * B], w_up[n][:, k, P * m:P * (m + 1)],
                                       shift[:, k, n, :], start=(k == 0), stop=(k == KD - 1))
                mm.then_inc(up_bias_summed, 1)

            def keep_warm(n):
                for _ in range(n):
                    pe.matmul(ps_up[1][:, :], zeros[:, 0:P], zeros[:, :], start=True, stop=True)

            pe.wait_ge(ident_ready, 1)
            pe.wait_ge(zeros_ready, 1)
            pe.wait_ge(cond_loaded, 16)
            for k in range(KD):
                mm = pe.transpose(ps_cond[:, B * k:B * (k + 1)], cond_rows[:, P * k:P * (k + 1)], ident[0:B, 0:B])
            mm.then_inc(cond_transposed, 1)
            keep_warm(6)
            pe.wait_ge(silu_ready, 1)
            modulation(0, SCALE, ps_scale[0], scale_summed)
            for n in range(3):
                pe.wait_ge(biases_loaded[n], 16)
            pe.transpose(ps_bias, bias_rows[:, :], ident[0:ROWS, 0:ROWS]).then_inc(bias_transposed, 1)
            transpose_xhat(0, first=True)
            pe.wait_ge(bias_ready, 1)
            modulation(0, SHIFT, ps_shift[0], shift_summed)
            gates(0)
            pe.wait_ge(w_up_hi_ready[0], 1)
            pe.wait_ge(w_up_lo_ready[0], 1)

            def step(layer, i, down_layer=None, last=False, first=False, first_down=False):
                early = M[layer] // 2
                up(layer, i, range(M[0] // 2), first)
                if not last:
                    transpose_xhat(i + 1)
                up(layer, i, range(M[0] // 2, early), first)
                if down_layer is not None:
                    down(down_layer, i - 1, 0, first_down)
                up(layer, i, range(early, M[0]), first)
                up(layer, i, range(M[0], M[layer]), first or (layer == 1 and isinstance(i, int) and i == NG))
                if down_layer is not None:
                    down(down_layer, i - 1, 1, first_down)

            up(0, 0, [0], True)
            pe.wait_ge(scale_ready, 1)
            shift_product(0)
            up(0, 0, [1], True)
            transpose_xhat(1)
            modulation(1, SCALE, ps_scale[1], scale_summed)
            modulation(1, SHIFT, ps_shift[1], shift_summed)
            pe.wait_ge(gates_ready, 1)
            gates(1)
            pe.wait_ge(w_down_hi_ready[0], 1)
            pe.wait_ge(w_down_lo_ready[0], 1)
            pe.wait_ge(up_bias_ready, 1)
            pe.wait_ge(scale_ready, 2)
            step(0, 1, 0, first_down=True)
            pe.wait_ge(w_up_loaded[1], 16)
            shift_product(1)
            with pe.Fori(2, NG) as i:
                step(0, i, 0)
            pe.wait_ge(w_up_hi_ready[1], 1)
            pe.wait_ge(w_up_lo_ready[1], 1)
            pe.wait_ge(up_bias_ready, 2)
            pe.wait_ge(gates_ready, 2)
            step(1, NG, 0)
            pe.wait_ge(w_down_hi_ready[1], 1)
            pe.wait_ge(w_down_lo_ready[1], 1)
            with pe.Fori(NG + 1, LAST) as i:
                step(1, i, 1)
            step(1, LAST, 1, last=True)
            for t in range(TILES):
                if t < 2:
                    pe.wait_ge(gelu_done[t], HALVES * runs(t, LAST + 1))
                else:
                    pe.wait_ge(norm_lo_ready, HALVES * KD * (LAST + 1))
                down_tile(1, LAST, t, ps_last[t]).then_inc(last_down_done, 1)


_INS = ['x', 'cond_1024', 'L0_cond_ada_w', 'L0_cond_ada_b', 'L0_cond_ssm_w1', 'L0_cond_ssm_b1', 'L0_cond_ssm_w2',
        'L0_cond_ssm_b2', 'L0_cond_ff_w1', 'L0_cond_ff_b1', 'L0_cond_ff_w2', 'L0_cond_ff_b2']


def kernel(**inputs):
    import numpy as _np
    import concourse.bacc as _bacc
    from concourse import mybir as _mybir
    from concourse.bass_utils import run_bass_kernel_spmd as _run

    nc = _bacc.Bacc("TRN2", target_bir_lowering=False, num_devices=1)
    arrays, args = {}, []
    for name in _INS:
        a = _np.ascontiguousarray(inputs[name])
        arrays[f"in_{name}_dram"] = a
        args.append(nc.dram_tensor(f"in_{name}_dram", a.shape, _mybir.dt.from_np(a.dtype), kind="ExternalInput").ap())
    B, _, D = arrays["in_x_dram"].shape
    args.append(nc.dram_tensor("gate_scratch", (B, 2, D), _mybir.dt.float32, kind="Internal").ap())
    args.append(nc.dram_tensor("out_0_dram", arrays["in_x_dram"].shape, _mybir.dt.float32, kind="ExternalOutput").ap())
    conditioned_block_kernel(nc, *args)
    r = _run(nc, [arrays], core_ids=[0])
    return r.results[0]["out_0_dram"]
```

```python
from contextlib import ExitStack

import concourse.bass as bass
from concourse import mybir

ALU = mybir.AluOpType
ACT = mybir.ActivationFunctionType
F32 = mybir.dt.float32
F32R = mybir.dt.float32r

P = 128
EPS = 1e-6
HALVES = 2


def conditioned_block_kernel(
    nc: bass.Bass,
    x: bass.AP,
    cond: bass.AP,
    ada_w: bass.AP,
    biases: bass.AP,
    gate_b: bass.AP,
    w1: bass.AP,
    w2: bass.AP,
    b2: bass.AP,
    ff_w1: bass.AP,
    ff_w2: bass.AP,
    ff_b2: bass.AP,
    gate_scratch: bass.AP,
    out: bass.AP,
):
    B, S, D = x.shape
    KD = D // P
    CT = S // P
    NG = B // HALVES
    TILES = HALVES * CT
    GT = TILES * P
    HT = CT * P
    HIDDEN = (w1.shape[2], ff_w1.shape[2])
    M = tuple(h // P for h in HIDDEN)
    MMAX = max(M)
    LAST = 2 * NG - 1
    assert (S, D, GT, HIDDEN) == (256, 256, 512, (256, 512))

    COL_B1 = (6 * KD, 6 * KD + M[0])
    SHIFT, SCALE, GATE = range(3)

    with ExitStack() as ctx:
        def sb(name, shape, dt=F32):
            return ctx.enter_context(nc.sbuf_tensor(name, shape, dt))

        def psum(name, shape):
            return ctx.enter_context(nc.psum_tensor(name, shape, F32))

        def sem(name):
            return ctx.enter_context(nc.semaphore(name))

        xres = sb("xres", [P, NG, TILES, D])
        xhat = sb("xhat", [P, TILES, D])
        stats = sb("stats", [P, 2 * NG, TILES, 6])
        meanvar = sb("meanvar", [P, 2 * NG, TILES, 2])
        vareps = sb("vareps", [P, 2 * NG, TILES])
        rstd = sb("rstd", [P, 2 * NG, TILES])
        mean_rstd = sb("mean_rstd", [P, 2 * NG, TILES])
        minus_half = sb("minus_half", [P, TILES])
        ident = sb("ident", [P, P])

        norm_hi = sb("norm_hi", [P, NG, KD, GT], F32R)
        norm_lo = sb("norm_lo", [P, NG, KD, GT], F32R)
        h = sb("h", [P, MMAX, GT])
        h_hi = sb("h_hi", [P, MMAX, GT], F32R)
        h_lo = sb("h_lo", [P, MMAX, GT], F32R)
        branch = sb("branch", [P, HALVES, CT, D])
        gated_bias = sb("gated_bias", [P, HALVES, D])

        w_up = [sb(f"w_up{n}", [P, KD, HIDDEN[n]]) for n in range(2)]
        w_up_hi = [sb(f"w_up_hi{n}", [P, KD, HIDDEN[n]], F32R) for n in range(2)]
        w_up_lo = [sb(f"w_up_lo{n}", [P, KD, HIDDEN[n]], F32R) for n in range(2)]
        w_down = [sb(f"w_down{n}", [P, M[n], D]) for n in range(2)]
        w_down_hi = [sb(f"w_down_hi{n}", [P, M[n], D], F32R) for n in range(2)]
        w_down_lo = [sb(f"w_down_lo{n}", [P, M[n], D], F32R) for n in range(2)]

        cond_sb = sb("cond_sb", [P, KD, B])
        cond_silu = sb("cond_silu", [P, KD, B])
        ada_sb = sb("ada_sb", [P, 2, 3, KD, D])
        bias_cols = sb("bias_cols", [P, biases.shape[1]])
        shift = sb("shift", [P, KD, 2, B])
        scale = sb("scale", [P, KD, 2 * B])
        up_bias = [sb(f"up_bias{n}", [P, M[n], B]) for n in range(2)]
        gate_bias = sb("gate_bias", [B, 2, D])
        gate_rows = sb("gate_rows", [B, 2, D])
        gate = sb("gate", [P, 2 * B, D])
        down_bias = [sb(f"down_bias{n}", [P, D]) for n in range(2)]
        table_probe = sb("table_probe", [P, 3])
        zeros = sb("zeros", [P, 2 * P], mybir.dt.bfloat16)

        ps_tr = [psum(f"ps_tr{k}", [P, GT]) for k in range(KD)]
        ps_up = [psum(f"ps_up{m}", [P, GT]) for m in range(MMAX)]
        ps_down = [psum(f"ps_down{hb}", [P, CT, D]) for hb in range(HALVES)]
        ps_last = [bank[:, 0:D] for bank in (ps_up[0], ps_up[1], ps_tr[0], ps_tr[1])]
        ps_scale = [ps_down[0][:, 0, 64:64 + KD * B], ps_up[3][:, 0:KD * B]]
        ps_shift = [ps_up[3][:, 256:256 + KD * B], ps_up[3][:, 64:64 + KD * B]]
        ps_up_bias = [ps_down[0][:, 1, 0:M[0] * B], ps_up[3][:, 128:128 + M[1] * B]]
        ps_gate = [ps_up[2][0:B, D * n:D * (n + 1)] for n in range(2)]

        cond_loaded = sem("cond_loaded")
        biases_loaded = sem("biases_loaded")
        gate_bias_loaded = sem("gate_bias_loaded")
        ada_loaded = [[sem(f"ada_loaded{n}_{s}") for s in range(3)] for n in range(2)]
        x_loaded = [sem(f"x_loaded{b}") for b in range(B)]
        w_up_loaded = [sem(f"w_up_loaded{n}") for n in range(2)]
        w_down_loaded = [sem(f"w_down_loaded{n}") for n in range(2)]
        down_bias_loaded = sem("down_bias_loaded")
        gates_stored = [sem(f"gates_stored{n}") for n in range(2)]
        gates_loaded = [sem(f"gates_loaded{q}") for q in range(4)]
        out_stored = sem("out_stored")

        zeros_ready = sem("zeros_ready")
        ident_zeroed = sem("ident_zeroed")
        ident_ready = sem("ident_ready")
        constants_ready = sem("constants_ready")
        silu_ready = sem("silu_ready")
        scale_summed = sem("scale_summed")
        shift_summed = sem("shift_summed")
        gate_summed = sem("gate_summed")
        up_bias_summed = sem("up_bias_summed")
        scale_ready = sem("scale_ready")
        shift_ready = sem("shift_ready")
        up_bias_ready = sem("up_bias_ready")
        gates_ready = sem("gates_ready")

        stats_done = sem("stats_done")
        meanvar_done = sem("meanvar_done")
        vareps_done = sem("vareps_done")
        rstd_done = sem("rstd_done")
        mean_rstd_done = sem("mean_rstd_done")
        xhat_ready = sem("xhat_ready")
        transposed = sem("transposed")
        norm_hi_ready = sem("norm_hi_ready")
        norm_lo_ready = sem("norm_lo_ready")
        up_done = [sem(f"up_done{m}") for m in range(MMAX)]
        gelu_done = [sem(f"gelu_done{m}") for m in range(MMAX)]
        h_hi_ready = [sem(f"h_hi_ready{q}") for q in range(MMAX // 2)]
        h_lo_ready = [sem(f"h_lo_ready{q}") for q in range(MMAX // 2)]
        down_done = sem("down_done")
        biased = sem("biased")
        gated = sem("gated")
        residual_done = sem("residual_done")
        bias_gated = sem("bias_gated")
        last_down_done = sem("last_down_done")
        last_gated = sem("last_gated")
        last_residual = sem("last_residual")
        w_up_hi_ready = [sem(f"w_up_hi_ready{n}") for n in range(2)]
        w_up_lo_ready = [sem(f"w_up_lo_ready{n}") for n in range(2)]
        w_down_hi_ready = [sem(f"w_down_hi_ready{n}") for n in range(2)]
        w_down_lo_ready = [sem(f"w_down_lo_ready{n}") for n in range(2)]

        def runs(m, i):
            return i if m < M[0] else i - NG

        def pair_ready(m):
            return h_lo_ready[m // 2]

        block = ctx.enter_context(nc.Block())

        def load_ada(eng, n, s):
            eng.dma_start(ada_sb[:, n, s], ada_w[:, n, s]).then_inc(ada_loaded[n][s], 16)

        def load_x(eng, b):
            g, hb = b // HALVES, b % HALVES
            eng.dma_start(xres[:, g, CT * hb:CT * (hb + 1), :].rearrange("p c f -> p (c f)"),
                          x[b].rearrange("(p c) f -> p (c f)", c=CT)).then_inc(x_loaded[b], 16)

        def load_w(eng, dst, w, signal):
            eng.dma_start(dst[:, :, :], w).then_inc(signal, 16)

        @block.sync
        def _(sp):
            def store_gates(n):
                sp.wait_ge(gates_ready, n + 1)
                sp.dma_start(gate_scratch[:, n, :], gate_rows[:, n, :]).then_inc(gates_stored[n], 16)

            def broadcast_gates(n):
                sp.wait_ge(gates_stored[n], 16)
                for half in (slice(0, B // 2), slice(B // 2, B)):
                    sp.dma_start(gate[:, B * n + half.start:B * n + half.stop, :],
                                 gate_scratch[half, n, :].rearrange("(a b) f -> a b f", a=1
                                                                    ).to_broadcast([P, B // 2, D])
                                 ).then_inc(gates_loaded[2 * n + half.start // (B // 2)], 16)

            load_x(sp, 0)
            load_x(sp, 1)
            load_ada(sp, 0, SCALE)
            sp.dma_start(bias_cols[:, :], biases).then_inc(biases_loaded, 16)
            load_w(sp, w_up[0], w1, w_up_loaded[0])
            load_x(sp, 2)
            load_ada(sp, 0, SHIFT)
            load_x(sp, 3)
            load_ada(sp, 0, GATE)
            load_w(sp, w_down[0], w2, w_down_loaded[0])
            load_x(sp, 4)
            load_x(sp, 5)
            load_x(sp, 6)
            load_x(sp, 7)
            load_ada(sp, 1, GATE)
            load_ada(sp, 1, SCALE)
            load_ada(sp, 1, SHIFT)
            load_w(sp, w_up[1], ff_w1, w_up_loaded[1])
            for n, b in enumerate((b2, ff_b2)):
                sp.dma_start(down_bias[n][:, :], b.rearrange("(a f) -> a f", a=1).to_broadcast([P, D])
                             ).then_inc(down_bias_loaded, 16)
            load_w(sp, w_down[1], ff_w2, w_down_loaded[1])
            for n in range(2):
                store_gates(n)
                broadcast_gates(n)

            for i in range(NG, LAST):
                for hb in range(HALVES):
                    b = HALVES * (i - NG) + hb
                    sp.wait_ge(residual_done, HALVES * i + hb + 1)
                    sp.dma_start(out[b].rearrange("(p c) f -> p (c f)", c=CT),
                                 xres[:, i - NG, CT * hb:CT * (hb + 1), :].rearrange("p c f -> p (c f)")
                                 ).then_inc(out_stored, 16)
            for t in range(TILES):
                hb, c = t // CT, t % CT
                sp.wait_ge(last_residual, t + 1)
                sp.dma_start(out[HALVES * (NG - 1) + hb].rearrange("(p c) f -> p c f", c=CT)[:, c, :],
                             xres[:, NG - 1, t, :]).then_inc(out_stored, 16)
            sp.wait_ge(out_stored, 16 * (HALVES * (NG - 1) + TILES))

        @block.scalar
        def _(act):
            act.dma_start(cond_sb[:, :, :], cond).then_inc(cond_loaded, 16)
            act.wait_ge(constants_ready, 1)
            act.activation(table_probe[:, 0:1], minus_half[:, 0:1], ACT.Silu)
            act.wait_ge(cond_loaded, 16)
            act.activation(cond_silu[:, :, :], cond_sb[:, :, :], ACT.Silu).then_inc(silu_ready, 1)
            act.activation(table_probe[:, 1:2], minus_half[:, 0:1], ACT.Gelu)

            def split_weight(dst, src, loaded, ready):
                act.wait_ge(loaded, 16)
                act.activation(dst[:, :, :], src[:, :, :], ACT.Identity).then_inc(ready, 1)

            def normalise(layer, i, count):
                g = i - NG * layer
                act.wait_ge(mean_rstd_done, count)
                act.wait_ge(transposed, KD * i)
                for t in range(TILES):
                    act.activation(xhat[:, t, :], xres[:, bass.ds(g, 1), t, :].rearrange("p a f -> p (a f)"),
                                   ACT.Identity, bias=mean_rstd[:, i, t:t + 1], scale=rstd[:, i, t:t + 1]
                                   ).then_inc(xhat_ready, 1)

            def split_norm(i, reused):
                g = i - NG * reused
                for k in range(KD):
                    act.wait_ge(transposed, KD * i + k + 1)
                    if reused:
                        act.wait_ge(up_done[M[0] - 1], i - NG + 1)
                    for hb in range(HALVES):
                        cols = slice(HT * hb, HT * (hb + 1))
                        act.activation(norm_hi[:, bass.ds(g, 1), k, cols].rearrange("p a n -> p (a n)"),
                                       ps_tr[k][:, cols], ACT.Identity,
                                       scale=scale[:, k, bass.ds(HALVES * i + hb, 1)]).then_inc(norm_hi_ready, 1)

            def gelu(layer, i, chunks, first):
                func = (ACT.Gelu, ACT.Gelu_apprx_tanh)[layer]
                for m in chunks:
                    act.wait_ge(up_done[m], runs(m, i) + 1)
                    if not first:
                        act.wait_ge(pair_ready(m), HALVES * runs(m, i))
                    for hb in range(HALVES):
                        cols = slice(HT * hb, HT * (hb + 1))
                        b = HALVES * (i - NG * layer) + hb
                        act.activation(h[:, m, cols], ps_up[m][:, cols], func,
                                       bias=up_bias[layer][:, m, bass.ds(b, 1)]).then_inc(gelu_done[m], 1)

            def split_h(layer, i, hb, m, first=False):
                cols = slice(HT * hb, HT * (hb + 1))
                if not first:
                    act.wait_ge(down_done, HALVES * (i - 1) + hb + 1)
                act.wait_ge(gelu_done[m + 1], HALVES * (runs(m, i) + 1))
                act.activation(h_hi[:, m:m + 2, cols], h[:, m:m + 2, cols], ACT.Identity
                               ).then_inc(h_hi_ready[m // 2], 1)

            def narrow_step(i, first=False, norm_reused=False):
                gelu(0, i, [0], first)
                split_norm(i + 1, norm_reused)
                gelu(0, i, [1], first)
                for hb in range(HALVES):
                    split_h(0, i, hb, 0, first)

            def wide_step(i, last=False):
                first = isinstance(i, int) and i == NG
                gelu(1, i, [0, 1], False)
                if not last:
                    split_norm(i + 1, True)
                split_h(1, i, 0, 0)
                gelu(1, i, [2, 3], first)
                split_h(1, i, 0, 2)
                split_h(1, i, 1, 0)
                split_h(1, i, 1, 2)

            split_weight(w_up_hi[0], w_up[0], w_up_loaded[0], w_up_hi_ready[0])
            act.wait_ge(scale_ready, 1)
            split_norm(0, False)
            split_weight(w_down_hi[0], w_down[0], w_down_loaded[0], w_down_hi_ready[0])
            normalise(0, 1, 1)
            act.wait_ge(up_bias_ready, 1)
            narrow_step(0, first=True)
            split_weight(w_up_hi[1], w_up[1], w_up_loaded[1], w_up_hi_ready[1])
            narrow_step(1)
            normalise(0, 3, 2)
            narrow_step(2)
            normalise(1, 4, 3)
            act.wait_ge(scale_ready, 2)
            narrow_step(3, norm_reused=True)
            act.wait_ge(up_bias_ready, 2)
            act.activation(table_probe[:, 2:3], minus_half[:, 0:1], ACT.Gelu_apprx_tanh)
            split_weight(w_down_hi[1], w_down[1], w_down_loaded[1], w_down_hi_ready[1])
            wide_step(NG)
            with act.Fori(NG + 1, LAST) as i:
                wide_step(i)
            wide_step(LAST, last=True)

        @block.vector
        def _(dve):
            def ln_sums(layer, i, tiles=range(TILES)):
                g = i - NG * layer
                for t in tiles:
                    if t % CT == 0:
                        if layer == 0:
                            dve.wait_ge(x_loaded[HALVES * i + t // CT], 16)
                        else:
                            dve.wait_ge(residual_done, HALVES * g + t // CT + 1)
                    dve.bn_stats(stats[:, i, t, :], xres[:, bass.ds(g, 1), t, :].rearrange("p a f -> p (a f)")
                                 ).then_inc(stats_done, 1)

            def ln_variance(layer, i, tiles=range(TILES)):
                for t in tiles:
                    dve.wait_ge(stats_done, TILES * i + t + 1)
                    dve.bn_aggr(meanvar[:, i, t, :], stats[:, i, t, :]).then_inc(meanvar_done, 1)
                dve.wait_ge(meanvar_done, TILES * i + tiles.stop)
                span = slice(tiles.start, tiles.stop)
                dve.tensor_scalar(vareps[:, i, span], meanvar[:, i, span, 1], EPS, None, ALU.add
                                  ).then_inc(vareps_done, 1)

            def ln_stats(layer, i):
                ln_sums(layer, i)
                ln_variance(layer, i)

            def ln_offset(i):
                dve.wait_ge(rstd_done, HALVES + i)
                dve.scalar_tensor_tensor(mean_rstd[:, i, :], meanvar[:, i, :, 0], -1.0, rstd[:, i, :],
                                         ALU.mult, ALU.mult).then_inc(mean_rstd_done, 1)

            def normalise(layer, i, tiles=range(TILES)):
                g = i - NG * layer
                if i == 0:
                    dve.wait_ge(rstd_done, tiles.stop // CT)
                else:
                    dve.wait_ge(rstd_done, HALVES + i)
                    dve.wait_ge(transposed, KD * i)
                for t in tiles:
                    dve.tensor_scalar(xhat[:, t, :], xres[:, bass.ds(g, 1), t, :].rearrange("p a f -> p (a f)"),
                                      meanvar[:, i, t, 0:1], rstd[:, i, t:t + 1],
                                      ALU.subtract, ALU.mult).then_inc(xhat_ready, 1)

            def split_norm(i, reused, chunks=range(KD)):
                g = i - NG * reused
                for k in chunks:
                    dve.wait_ge(norm_hi_ready, HALVES * (KD * i + k + 1))
                    for hb in range(HALVES):
                        cols = slice(HT * hb, HT * (hb + 1))
                        dve.scalar_tensor_tensor(
                            norm_lo[:, bass.ds(g, 1), k, cols].rearrange("p a n -> p (a n)"), ps_tr[k][:, cols],
                            scale[:, k, bass.ds(HALVES * i + hb, 1)],
                            norm_hi[:, bass.ds(g, 1), k, cols].rearrange("p a n -> p (a n)").bitcast(F32),
                            ALU.mult, ALU.subtract).then_inc(norm_lo_ready, 1)

            def split_h(layer, i, hb):
                cols = slice(HT * hb, HT * (hb + 1))
                for m in range(0, M[layer], 2):
                    dve.wait_ge(h_hi_ready[m // 2], HALVES * runs(m, i) + hb + 1)
                    dve.tensor_tensor(h_lo[:, m:m + 2, cols], h[:, m:m + 2, cols],
                                      h_hi[:, m:m + 2, cols].bitcast(F32), ALU.subtract
                                      ).then_inc(h_lo_ready[m // 2], 1)

            def add_bias(layer, i, hb, first=False):
                dve.wait_ge(down_done, HALVES * i + hb + 1)
                if not first:
                    dve.wait_ge(residual_done, HALVES * (i - 1) + hb + 1)
                dve.tensor_tensor(branch[:, hb, :, :], ps_down[hb][:, :, :],
                                  down_bias[layer][:, :].rearrange("p (a f) -> p a f", a=1).to_broadcast([P, CT, D]),
                                  ALU.add).then_inc(biased, 1)

            def bias_of(col, chunks):
                return bias_cols[:, col:col + chunks].rearrange("p (k a) -> p k a", a=1).to_broadcast([P, chunks, B])

            def chunked(ps):
                return ps.rearrange("p (k b) -> p k b", b=B)

            def scale_of(n):
                dve.wait_ge(scale_summed, n + 1)
                if n == 1:
                    dve.wait_ge(shift_summed, 2)
                dve.scalar_tensor_tensor(scale[:, :, B * n:B * (n + 1)], chunked(ps_scale[n]), 1.0,
                                         bias_of(KD * (3 * n + SCALE), KD), ALU.add, ALU.add).then_inc(scale_ready, 1)

            def shift_of(n):
                dve.wait_ge(shift_summed, n + 1)
                dve.tensor_tensor(shift[:, :, n, :], chunked(ps_shift[n]),
                                  bias_of(KD * (3 * n + SHIFT), KD), ALU.add).then_inc(shift_ready, 1)

            def up_bias_of(n):
                dve.wait_ge(up_bias_summed, n + 1)
                dve.tensor_tensor(up_bias[n][:, :, :], chunked(ps_up_bias[n]), bias_of(COL_B1[n], M[n]),
                                  ALU.add).then_inc(up_bias_ready, 1)

            def gate_of(n):
                dve.wait_ge(gate_summed, n + 1)
                dve.tensor_tensor(gate_rows[:, n, :], ps_gate[n], gate_bias[:, n, :], ALU.add).then_inc(gates_ready, 1)

            dve.memset(zeros[:, :], 0.0).then_inc(zeros_ready, 1)
            first_half, second_half = range(0, CT), range(CT, TILES)
            ln_sums(0, 0, first_half)
            ln_variance(0, 0, first_half)
            ln_sums(0, 0, second_half)
            ln_variance(0, 0, second_half)
            normalise(0, 0, first_half)
            normalise(0, 0, second_half)
            ln_sums(0, 1, first_half)
            dve.wait_ge(biases_loaded, 16)
            scale_of(0)
            ln_sums(0, 1, second_half)
            ln_variance(0, 1)
            shift_of(0)
            split_norm(0, False, [0])
            ln_offset(1)
            split_norm(0, False, [1])
            ln_sums(0, 2)
            up_bias_of(0)
            ln_variance(0, 2)
            split_norm(1, False, [0])
            dve.wait_ge(gate_bias_loaded, 16)
            gate_of(0)
            split_norm(1, False, [1])
            normalise(0, 2)
            ln_stats(0, 3)
            dve.wait_ge(w_up_hi_ready[1], 1)
            dve.tensor_tensor(w_up_lo[1][:, :, :], w_up[1][:, :, :], w_up_hi[1][:, :, :].bitcast(F32), ALU.subtract
                              ).then_inc(w_up_lo_ready[1], 1)
            dve.wait_ge(down_bias_loaded, 32)
            add_bias(0, 0, 0, True)
            split_norm(2, False)
            ln_offset(3)
            split_h(0, 1, 0)
            add_bias(0, 0, 1, True)
            split_h(0, 1, 1)
            scale_of(1)
            shift_of(1)
            gate_of(1)

            def narrow_step(i, norm_reused):
                ln_stats(1, i + 2)
                add_bias(0, i - 1, 0)
                split_norm(i + 1, norm_reused, [0])
                if i == 2:
                    ln_offset(i + 2)
                split_norm(i + 1, norm_reused, [1])
                if i == 3:
                    normalise(1, i + 2)
                add_bias(0, i - 1, 1)
                split_h(0, i, 0)
                split_h(0, i, 1)

            def wide_step(i, down, ln=True, last=False):
                if ln:
                    ln_stats(1, i + 2)
                if not last:
                    split_norm(i + 1, True)
                add_bias(down, i - 1, 0)
                if ln:
                    normalise(1, i + 2)
                split_h(1, i, 0)
                add_bias(down, i - 1, 1)
                split_h(1, i, 1)

            narrow_step(2, norm_reused=False)
            up_bias_of(1)
            narrow_step(3, norm_reused=True)
            wide_step(4, 0)
            wide_step(5, 1)
            wide_step(6, 1, ln=False)
            wide_step(7, 1, ln=False, last=True)
            dve.wait_ge(bias_gated, 2 * HALVES)
            for t in range(TILES):
                hb, c = t // CT, t % CT
                if c == 0:
                    dve.wait_ge(residual_done, HALVES * (LAST - 1) + hb + 1)
                dve.wait_ge(last_down_done, t + 1)
                dve.tensor_tensor(branch[:, hb, c, :], ps_last[t], gate[:, HALVES * LAST + hb, :], ALU.mult
                                  ).then_inc(last_gated, 1)
                dve.wait_ge(last_gated, t + 1)
                dve.tensor_tensor(xres[:, NG - 1, t, :], xres[:, NG - 1, t, :], branch[:, hb, c, :], ALU.add
                                  ).then_inc(last_residual, 1)

        @block.gpsimd
        def _(pool):
            pool.memset(minus_half[:, :], -0.5).then_inc(constants_ready, 1)
            pool.memset(ident[:, :], 0.0).then_inc(ident_zeroed, 1)
            pool.wait_ge(ident_zeroed, 1)
            pool.affine_select(out=ident[:, :], in_=ident[:, :], compare_op=ALU.not_equal, fill=1.0, base=0,
                               pattern=[[-1, P]], channel_multiplier=1).then_inc(ident_ready, 1)
            pool.dma_start(gate_bias[:, :, :], gate_b.rearrange("(a l) n -> a l n", a=1).to_broadcast([B, 2, D])
                           ).then_inc(gate_bias_loaded, 16)

            def inverse_std(i):
                pool.wait_ge(vareps_done, HALVES + i)
                pool.tensor_tensor(rstd[:, i, :], vareps[:, i, :], minus_half[:, :], ALU.pow).then_inc(rstd_done, 1)

            def add_residual(layer, i, hb):
                g = i - NG * layer
                pool.wait_ge(biased, HALVES * i + hb + 1)
                pool.tensor_tensor(branch[:, hb, :, :], branch[:, hb, :, :],
                                   gate[:, bass.ds(HALVES * i + hb, 1), :].to_broadcast([P, CT, D]),
                                   ALU.mult).then_inc(gated, 1)
                pool.wait_ge(gated, HALVES * i + hb + 1)
                dst = xres[:, bass.ds(g, 1), CT * hb:CT * (hb + 1), :].rearrange("p a c f -> p (a c) f")
                pool.tensor_tensor(dst, dst, branch[:, hb, :, :], ALU.add).then_inc(residual_done, 1)

            def split_weight(dst, src, hi, hi_ready, ready):
                pool.wait_ge(hi_ready, 1)
                pool.tensor_tensor(dst[:, :, :], src[:, :, :], hi[:, :, :].bitcast(F32),
                                   ALU.subtract).then_inc(ready, 1)

            def split_h(i, hb):
                cols = slice(HT * hb, HT * (hb + 1))
                pool.wait_ge(h_hi_ready[0], HALVES * i + hb + 1)
                pool.tensor_tensor(h_lo[:, 0:2, cols], h[:, 0:2, cols], h_hi[:, 0:2, cols].bitcast(F32),
                                   ALU.subtract).then_inc(h_lo_ready[0], 1)

            pool.wait_ge(constants_ready, 1)
            for hb in range(HALVES):
                tiles = slice(CT * hb, CT * (hb + 1))
                pool.wait_ge(vareps_done, hb + 1)
                pool.tensor_tensor(rstd[:, 0, tiles], vareps[:, 0, tiles], minus_half[:, tiles], ALU.pow
                                   ).then_inc(rstd_done, 1)
            split_weight(w_up_lo[0], w_up[0], w_up_hi[0], w_up_hi_ready[0], w_up_lo_ready[0])
            inverse_std(1)
            split_weight(w_down_lo[0], w_down[0], w_down_hi[0], w_down_hi_ready[0], w_down_lo_ready[0])
            inverse_std(2)
            split_h(0, 0)
            split_h(0, 1)
            inverse_std(3)

            def step(i, down, ln=True):
                if ln:
                    inverse_std(i + 2)
                for hb in range(HALVES):
                    add_residual(down, i - 1, hb)

            pool.wait_ge(gates_loaded[0], 16)
            step(1, 0, ln=False)
            step(2, 0)
            pool.wait_ge(gates_loaded[1], 16)
            step(3, 0)
            split_weight(w_down_lo[1], w_down[1], w_down_hi[1], w_down_hi_ready[1], w_down_lo_ready[1])
            step(4, 0)
            pool.wait_ge(gates_loaded[2], 16)
            pool.wait_ge(gates_loaded[3], 16)
            step(5, 1)
            pool.wait_ge(down_bias_loaded, 32)
            pool.wait_ge(xhat_ready, TILES * (LAST + 1))
            for hb in range(HALVES):
                pool.tensor_tensor(gated_bias[:, hb, :], gate[:, HALVES * LAST + hb, :], down_bias[1][:, :], ALU.mult
                                   ).then_inc(bias_gated, 1)
                pool.wait_ge(bias_gated, 2 * hb + 1)
                dst = xres[:, NG - 1, CT * hb:CT * (hb + 1), :]
                pool.tensor_tensor(dst, dst, gated_bias[:, hb:hb + 1, :].to_broadcast([P, CT, D]), ALU.add
                                   ).then_inc(bias_gated, 1)
            with pool.Fori(LAST - 1, LAST + 1) as i:
                step(i, 1, ln=False)

        @block.tensor
        def _(pe):
            def transpose_xhat(i, first=False):
                for k in range(KD):
                    if not first:
                        pe.wait_ge(norm_lo_ready, HALVES * (KD * (i - 1) + k + 1))
                    for t in range(TILES):
                        if k == 0:
                            pe.wait_ge(xhat_ready, TILES * i + t + 1)
                        mm = pe.transpose(ps_tr[k][:, P * t:P * (t + 1)], xhat[:, t, P * k:P * (k + 1)], ident[:, :])
                    mm.then_inc(transposed, 1)

            def up_hi(layer, i, m, first=False):
                g, cols = i - NG * layer, slice(P * m, P * (m + 1))
                if not first:
                    pe.wait_ge(gelu_done[m], HALVES * runs(m, i))
                for k in range(KD):
                    hi = norm_hi[:, bass.ds(g, 1), k, :].rearrange("p a n -> p (a n)")
                    if m == 0:
                        pe.wait_ge(norm_hi_ready, HALVES * (KD * i + k + 1))
                    pe.matmul(ps_up[m][:, :], w_up_lo[layer][:, k, cols], hi, start=(k == 0), stop=False)
                    pe.matmul(ps_up[m][:, :], w_up_hi[layer][:, k, cols], hi, start=False, stop=False)

            def up_lo(layer, i, m):
                g, cols = i - NG * layer, slice(P * m, P * (m + 1))
                for k in range(KD):
                    lo = norm_lo[:, bass.ds(g, 1), k, :].rearrange("p a n -> p (a n)")
                    if m == 0:
                        pe.wait_ge(norm_lo_ready, HALVES * (KD * i + k + 1))
                    mm = pe.matmul(ps_up[m][:, :], w_up_hi[layer][:, k, cols], lo, start=False, stop=(k == KD - 1))
                mm.then_inc(up_done[m], 1)

            def up(layer, i, chunks, first=False):
                for m in chunks:
                    up_hi(layer, i, m, first)
                    up_lo(layer, i, m)

            def down_tile(layer, i, t, dst):
                hb, rows = t // CT, slice(P * t, P * (t + 1))
                for m in range(M[layer]):
                    if t % CT == 0 and m % 2 == 0:
                        pe.wait_ge(pair_ready(m), HALVES * runs(m, i) + hb + 1)
                    pe.matmul(dst, h_hi[:, m, rows], w_down_hi[layer][:, m, :], start=(m == 0), stop=False)
                    pe.matmul(dst, h_hi[:, m, rows], w_down_lo[layer][:, m, :], start=False, stop=False)
                    mm = pe.matmul(dst, h_lo[:, m, rows], w_down_hi[layer][:, m, :],
                                   start=False, stop=(m == M[layer] - 1))
                return mm

            def down(layer, i, hb, first=False):
                if not first:
                    pe.wait_ge(biased, HALVES * (i - 1) + hb + 1)
                for c in range(CT):
                    mm = down_tile(layer, i, CT * hb + c, ps_down[hb][:, c, :])
                mm.then_inc(down_done, 1)

            def modulation(n, part, dst, signal):
                pe.wait_ge(ada_loaded[n][part], 16)
                for j in range(KD):
                    for k in range(KD):
                        mm = pe.matmul(dst[:, j * B:(j + 1) * B], ada_sb[:, n, part, k, P * j:P * (j + 1)],
                                       cond_silu[:, k, :], start=(k == 0), stop=(k == KD - 1))
                mm.then_inc(signal, 1)

            def gates(n):
                pe.wait_ge(ada_loaded[n][GATE], 16)
                for k in range(KD):
                    mm = pe.matmul(ps_gate[n], cond_silu[:, k, :], ada_sb[:, n, GATE, k, :],
                                   start=(k == 0), stop=(k == KD - 1))
                mm.then_inc(gate_summed, 1)

            def shift_product(n):
                pe.wait_ge(shift_ready, n + 1)
                for m in range(M[n]):
                    for k in range(KD):
                        mm = pe.matmul(ps_up_bias[n][:, m * B:(m + 1) * B], w_up[n][:, k, P * m:P * (m + 1)],
                                       shift[:, k, n, :], start=(k == 0), stop=(k == KD - 1))
                mm.then_inc(up_bias_summed, 1)

            def keep_warm(n):
                for _ in range(n):
                    pe.matmul(ps_up[1][:, 0:2 * P], zeros[:, 0:P], zeros[:, :], start=True, stop=True)

            pe.wait_ge(zeros_ready, 1)
            keep_warm(23)
            pe.wait_ge(silu_ready, 1)
            modulation(0, SCALE, ps_scale[0], scale_summed)
            pe.wait_ge(ident_ready, 1)
            keep_warm(1)
            transpose_xhat(0, first=True)
            modulation(0, SHIFT, ps_shift[0], shift_summed)
            pe.wait_ge(w_up_hi_ready[0], 1)
            pe.wait_ge(w_up_lo_ready[0], 1)

            def narrow_step(i):
                up(0, i, [0])
                down(0, i - 1, 0)
                transpose_xhat(i + 1)
                up(0, i, [1])
                down(0, i - 1, 1)

            def wide_step(i, down_layer, last=False):
                first = isinstance(i, int) and i == NG
                up(1, i, range(M[0]))
                if not last:
                    transpose_xhat(i + 1)
                down(down_layer, i - 1, 0)
                up(1, i, range(M[0], M[1]), first)
                down(down_layer, i - 1, 1)

            for m in range(M[0]):
                up_hi(0, 0, m, first=True)
            pe.wait_ge(scale_ready, 1)
            shift_product(0)
            for m in range(M[0]):
                up_lo(0, 0, m)
            transpose_xhat(1)
            gates(0)

            up_hi(0, 1, 0)
            modulation(1, SCALE, ps_scale[1], scale_summed)
            up_lo(0, 1, 0)
            modulation(1, SHIFT, ps_shift[1], shift_summed)
            pe.wait_ge(up_bias_ready, 1)
            pe.wait_ge(w_down_hi_ready[0], 1)
            pe.wait_ge(w_down_lo_ready[0], 1)
            down(0, 0, 0, first=True)
            transpose_xhat(2)
            up(0, 1, [1])
            down(0, 0, 1, first=True)
            pe.wait_ge(gates_ready, 1)
            gates(1)

            narrow_step(2)
            pe.wait_ge(w_up_loaded[1], 16)
            pe.wait_ge(scale_ready, 2)
            shift_product(1)
            narrow_step(3)

            pe.wait_ge(w_up_hi_ready[1], 1)
            pe.wait_ge(w_up_lo_ready[1], 1)
            pe.wait_ge(up_bias_ready, 2)
            pe.wait_ge(gates_ready, 2)
            wide_step(NG, 0)
            pe.wait_ge(w_down_hi_ready[1], 1)
            pe.wait_ge(w_down_lo_ready[1], 1)
            with pe.Fori(NG + 1, LAST) as i:
                wide_step(i, 1)
            wide_step(LAST, 1, last=True)
            for t in range(TILES):
                if t < 2:
                    pe.wait_ge(gelu_done[t], HALVES * runs(t, LAST + 1))
                else:
                    pe.wait_ge(norm_lo_ready, HALVES * KD * (LAST + 1))
                down_tile(1, LAST, t, ps_last[t]).then_inc(last_down_done, 1)


def kernel(**inputs):
    import numpy as _np
    import concourse.bacc as _bacc
    from concourse import mybir as _mybir
    from concourse.bass_utils import run_bass_kernel_spmd as _run

    x, cond = inputs["x"], inputs["cond_1024"]
    B, _, D = x.shape
    KD = D // P

    def chunks_inside(w):
        return _np.asarray(w).reshape(-1, P, w.shape[1]).transpose(1, 0, 2)

    ada_b = _np.asarray(inputs["L0_cond_ada_b"])
    biases = _np.concatenate([ada_b, inputs["L0_cond_ssm_b1"], inputs["L0_cond_ff_b1"]])
    laid_out = {
        "x": x,
        "cond": _np.asarray(cond).reshape(B, KD, P).transpose(2, 1, 0),
        "ada_w": _np.asarray(inputs["L0_cond_ada_w"]).reshape(KD, P, 2, 3, D).transpose(1, 2, 3, 0, 4),
        "biases": biases.reshape(-1, P).transpose(1, 0),
        "gate_b": ada_b.reshape(2, 3, D)[:, 2],
        "w1": chunks_inside(inputs["L0_cond_ssm_w1"]),
        "w2": chunks_inside(inputs["L0_cond_ssm_w2"]),
        "b2": inputs["L0_cond_ssm_b2"],
        "ff_w1": chunks_inside(inputs["L0_cond_ff_w1"]),
        "ff_w2": chunks_inside(inputs["L0_cond_ff_w2"]),
        "ff_b2": inputs["L0_cond_ff_b2"],
    }

    nc = _bacc.Bacc("TRN2", target_bir_lowering=False, num_devices=1)
    arrays, args = {}, []
    for name, a in laid_out.items():
        a = _np.ascontiguousarray(a)
        arrays[f"in_{name}_dram"] = a
        args.append(nc.dram_tensor(f"in_{name}_dram", a.shape, _mybir.dt.from_np(a.dtype), kind="ExternalInput").ap())
    args.append(nc.dram_tensor("gate_scratch", (B, 2, D), _mybir.dt.float32, kind="Internal").ap())
    args.append(nc.dram_tensor("out_0_dram", arrays["in_x_dram"].shape, _mybir.dt.float32, kind="ExternalOutput").ap())
    conditioned_block_kernel(nc, *args)
    r = _run(nc, [arrays], core_ids=[0])
    return r.results[0]["out_0_dram"]
```
